# Optimizing a Trainium2 kernel written in Bass

```python
import numpy as np
import jax
import jax.numpy as jnp

def _softmax(x, axis=-1):
    return jax.nn.softmax(x, axis=axis)

def _gelu(x):
    return jax.nn.gelu(x, approximate=True)

def _silu(x):
    return jax.nn.silu(x)

def _sigmoid(x):
    return jax.nn.sigmoid(x)

def _layernorm(x, axis=-1, eps=1e-05):
    m = jnp.mean(x, axis=axis, keepdims=True)
    v = jnp.var(x, axis=axis, keepdims=True)
    return (x - m) / jnp.sqrt(v + eps)

def _scatter_add(tgt, idx, src, axis=0):
    return tgt.at[idx].add(src)

def _segment_sum(src, seg, n):
    return jax.ops.segment_sum(src, seg, n)
kernel_name = 'mk_vit_tower_postln_d1_tok_img256_r4_fcc871'

def setup_inputs(seed: int=0):
    np.random.seed(seed)
    _w = jnp.asarray

    def _rec_inputs():
        import jax
        import jax.numpy as jnp
        _rk = jax.random.key(seed)
        x = -7.10856e-05 + 0.999911 * jax.random.normal(jax.random.fold_in(_rk, 1), (8, 64, 128, 64), jnp.float32)
        return x
    x = _rec_inputs()

    def _L0_tok_setup():
        import jax, jax.numpy as jnp
        import numpy as np
        PATCH_LEN = 16
        STRIDE = 8
        PAD = 8
        key = jax.random.key(seed)
        k1, k2 = jax.random.split(key)
        x = jax.random.normal(k1, (32, 64, 128, 64), dtype=jnp.float32)
        in_feat = 64 * (PATCH_LEN // 2 + 1) * 2
        W = jax.random.normal(k2, (64, in_feat), dtype=jnp.float32) * 0.02
        return {'x': x, 'W': W}
    _L0_tok_all = _L0_tok_setup()
    _L0_tok_in = {k: v for k, v in _L0_tok_all.items() if k in ('W',)}
    del _L0_tok_all

    def _L0_attn_setup():
        import jax, jax.numpy as jnp
        import numpy as np
        key = jax.random.key(seed)
        k1, k2, k3 = jax.random.split(key, 3)
        b, n_t, n, n_h = (8, 256, 64, 8)
        s = jax.random.normal(k1, (b, n_t, n), dtype=jnp.float32)
        Q = jax.random.normal(k2, (n_h, n, n), dtype=jnp.float32) * 0.02
        E = jax.random.normal(k3, (n_h, n, n), dtype=jnp.float32) * 0.02
        return {'s': s, 'Q': Q, 'E': E}
    _L0_attn_all = _L0_attn_setup()
    _L0_attn_in = {k: v for k, v in _L0_attn_all.items() if k in ('Q', 'E')}
    del _L0_attn_all

    def _L0_ffn_setup():
        import jax, jax.numpy as jnp
        import numpy as np
        BN_EPS = 0.001

        def _bn(h, g, b, m, v):
            return g * (h - m) * jax.lax.rsqrt(v + BN_EPS) + b
        key = jax.random.key(seed)
        ks = jax.random.split(key, 8)
        B, F, Df = (64, 64, 64)
        E, H, D = (8, 64, 64)
        s1 = 1.0 / np.sqrt(Df)
        s2 = 1.0 / np.sqrt(H)
        return {'x': jax.random.normal(ks[0], (B, F, Df), jnp.float32), 'Wr': jax.random.normal(ks[1], (Df, E), jnp.float32) * s1, 'br': jnp.zeros((E,), jnp.float32), 'W1': jax.random.normal(ks[2], (E, Df, H), jnp.float32) * s1, 'b1': jnp.zeros((E, H), jnp.float32), 'g1': jnp.ones((E, H), jnp.float32), 'be1': jnp.zeros((E, H), jnp.float32), 'm1': jnp.zeros((E, H), jnp.float32), 'v1': jnp.ones((E, H), jnp.float32), 'W2': jax.random.normal(ks[3], (E, H, H), jnp.float32) * s2, 'b2': jnp.zeros((E, H), jnp.float32), 'g2': jnp.ones((E, H), jnp.float32), 'be2': jnp.zeros((E, H), jnp.float32), 'm2': jnp.zeros((E, H), jnp.float32), 'v2': jnp.ones((E, H), jnp.float32), 'Wo': jax.random.normal(ks[4], (E, H, D), jnp.float32) * s2, 'bo': jnp.zeros((E, D), jnp.float32)}
    _L0_ffn_all = _L0_ffn_setup()
    _L0_ffn_in = {k: v for k, v in _L0_ffn_all.items() if k in ('Wr', 'br', 'W1', 'b1', 'g1', 'be1', 'm1', 'v1', 'W2', 'b2', 'g2', 'be2', 'm2', 'v2', 'Wo', 'bo')}
    del _L0_ffn_all
    return {'x': x, 'L0_tok_W': _L0_tok_in['W'], 'L0_attn_Q': _L0_attn_in['Q'], 'L0_attn_E': _L0_attn_in['E'], 'L0_ffn_Wr': _L0_ffn_in['Wr'], 'L0_ffn_br': _L0_ffn_in['br'], 'L0_ffn_W1': _L0_ffn_in['W1'], 'L0_ffn_b1': _L0_ffn_in['b1'], 'L0_ffn_g1': _L0_ffn_in['g1'], 'L0_ffn_be1': _L0_ffn_in['be1'], 'L0_ffn_m1': _L0_ffn_in['m1'], 'L0_ffn_v1': _L0_ffn_in['v1'], 'L0_ffn_W2': _L0_ffn_in['W2'], 'L0_ffn_b2': _L0_ffn_in['b2'], 'L0_ffn_g2': _L0_ffn_in['g2'], 'L0_ffn_be2': _L0_ffn_in['be2'], 'L0_ffn_m2': _L0_ffn_in['m2'], 'L0_ffn_v2': _L0_ffn_in['v2'], 'L0_ffn_Wo': _L0_ffn_in['Wo'], 'L0_ffn_bo': _L0_ffn_in['bo']}

def reference(x, L0_tok_W, L0_attn_Q, L0_attn_E, L0_ffn_Wr, L0_ffn_br, L0_ffn_W1, L0_ffn_b1, L0_ffn_g1, L0_ffn_be1, L0_ffn_m1, L0_ffn_v1, L0_ffn_W2, L0_ffn_b2, L0_ffn_g2, L0_ffn_be2, L0_ffn_m2, L0_ffn_v2, L0_ffn_Wo, L0_ffn_bo):
    import jax
    import jax.numpy as jnp

    def _L0_tok_ref(x, W):
        import jax, jax.numpy as jnp
        import numpy as np
        PATCH_LEN = 16
        STRIDE = 8
        PAD = 8
        B, C, T, V = x.shape
        xp = jnp.pad(x, ((0, 0), (0, 0), (0, PAD), (0, 0)), mode='edge')
        Tp = T + PAD
        N = (Tp - PATCH_LEN) // STRIDE + 1
        idx = jnp.arange(N)[:, None] * STRIDE + jnp.arange(PATCH_LEN)[None, :]
        patches = xp[:, :, idx, :]
        patches = jnp.transpose(patches, (0, 4, 2, 3, 1))
        xf = jnp.fft.rfft(patches, axis=-2, norm='ortho')
        F = xf.shape[-2]
        x_real = xf.real.reshape(B, V, N, F * C)
        x_imag = xf.imag.reshape(B, V, N, F * C)
        x_emb = jnp.concatenate([x_real, x_imag], axis=-1)
        x_emb = x_emb @ W.T
        return x_emb.reshape(B, V * N, -1)

    def _L0_attn_ref(s, Q, E):
        import jax, jax.numpy as jnp
        import numpy as np
        n_t = s.shape[1]
        qs = jnp.einsum('bti,hij->bhtj', s, Q)
        Omega = jnp.einsum('bhtj,buj->bhtu', qs, s)
        mask = jnp.tril(jnp.ones((n_t, n_t), dtype=s.dtype))
        Omega = Omega * mask
        es = jnp.einsum('hij,buj->bhui', E, s)
        r = jnp.einsum('bhtu,bhui->bti', Omega, es)
        return r

    def _L0_ffn_ref(x, Wr, br, W1, b1, g1, be1, m1, v1, W2, b2, g2, be2, m2, v2, Wo, bo):
        import jax, jax.numpy as jnp
        import numpy as np
        BN_EPS = 0.001

        def _bn(h, g, b, m, v):
            return g * (h - m) * jax.lax.rsqrt(v + BN_EPS) + b
        feat = jnp.mean(x, axis=0)
        w = jax.nn.softmax(feat @ Wr + br, axis=-1)
        h = jnp.einsum('bfd,edh->bfeh', x, W1) + b1
        h = jax.nn.relu(_bn(h, g1, be1, m1, v1))
        h = jnp.einsum('bfeh,ehk->bfek', h, W2) + b2
        h = jax.nn.relu(_bn(h, g2, be2, m2, v2))
        y = jnp.einsum('bfeh,ehd->bfed', h, Wo) + bo
        return jnp.einsum('bfed,fe->bfd', y, w)
    h = _L0_tok_ref(x, L0_tok_W)
    h = _layernorm(h + _L0_attn_ref(h, L0_attn_Q, L0_attn_E), axis=-1)
    h = _layernorm(h + _L0_ffn_ref(h, L0_ffn_Wr, L0_ffn_br, L0_ffn_W1, L0_ffn_b1, L0_ffn_g1, L0_ffn_be1, L0_ffn_m1, L0_ffn_v1, L0_ffn_W2, L0_ffn_b2, L0_ffn_g2, L0_ffn_be2, L0_ffn_m2, L0_ffn_v2, L0_ffn_Wo, L0_ffn_bo), axis=-1)
    return h

_drawn_inputs = setup_inputs


def setup_inputs(seed=0):
    import zlib

    import numpy as np

    out = dict(_drawn_inputs(seed))
    spreads = {'L0_ffn_br': (0.0, 0.1),
     'L0_ffn_b1': (0.0, 0.424),
     'L0_ffn_g1': (1.0, 0.2),
     'L0_ffn_be1': (0.0, 0.406),
     'L0_ffn_m1': (0.0, 0.44),
     'L0_ffn_v1': (1.0, 0.6),
     'L0_ffn_b2': (0.0, 0.309),
     'L0_ffn_g2': (1.0, 0.2),
     'L0_ffn_be2': (0.0, 0.343),
     'L0_ffn_m2': (0.0, 0.289),
     'L0_ffn_v2': (1.0, 0.6),
     'L0_ffn_bo': (0.0, 0.1)}
    factors = {}
    for name, (base, spread) in spreads.items():
        noise = np.random.default_rng([zlib.crc32(name.encode()), seed]).standard_normal(out[name].shape)
        drawn = base * np.exp(spread * noise) if base else spread * noise
        out[name] = jnp.asarray(drawn.astype(out[name].dtype))
    for name, factor in factors.items():
        out[name] = (out[name] * factor).astype(out[name].dtype)
    return out
```

```python
from contextlib import ExitStack

import concourse.bass as bass
from concourse import mybir

B, C, T, V = 8, 64, 128, 64
PATCH, STRIDE = 16, 8
NPATCH = T // STRIDE
FREQ = PATCH // 2 + 1
GF = 2 * FREQ
D = 64
NTOK = V * NPATCH
CH = 128
NC = NTOK // CH
HEADS = 8
HP = HEADS // 2
EXP = 8
EP = EXP // 2
GB = 4
NG = NC * B // GB
GT = GB * CH
QS = 4
NPAR = 10
LN_EPS = 1e-5
BN_EPS = 1e-3


def build(nc, x, tok_w, att_q, att_e, wr, br, w1, b1, g1, be1, m1, v1, w2, b2, g2, be2, m2, v2, wo, bo,
          dft, ident_in, mask_in, sel_in, out):
    f32, f32r = mybir.dt.float32, mybir.dt.float32r
    ALU, ACT, AX = mybir.AluOpType, mybir.ActivationFunctionType, mybir.AxisListType

    ctx = ExitStack()
    with ctx:
        def sb(name, shape, dt=f32, into=ctx):
            return into.enter_context(nc.sbuf_tensor(name, shape, dt))

        def sem(name):
            return ctx.enter_context(nc.semaphore(name))

        ident = sb("ident", [128, 128])
        mask = sb("mask", [128, CH])
        x1 = sb("x1", [128, NC, B, D])
        feat_half = sb("feat_half", [128, NG, D])
        w1_stack = sb("w1_stack", [128, EXP * D], f32r)
        w2_diag = sb("w2_diag", [128, EP, 128])
        wo_pair = sb("wo_pair", [128, EP, D])
        wr_sb = sb("wr_sb", [D, EXP])
        br_sb = sb("br_sb", [1, EXP])
        bo_sb = sb("bo_sb", [EXP, D])
        sel_sb = sb("sel_sb", [EXP, EP * 128])
        ones_row = sb("ones_row", [1, 128])
        par_rows = sb("par_rows", [NPAR * EP, 128])
        par = sb("par", [128, NPAR, EP])
        bn_scale = sb("bn_scale", [128, 2, EP])
        bn_bias = sb("bn_bias", [128, 2, EP])
        bn_tmp = sb("bn_tmp", [128, 2, EP])
        eps_ln = sb("eps_ln", [128, 1])
        eps_bn = sb("eps_bn", [128, 1])
        y_ln = sb("y_ln", [128, GB, D])
        xm_ln = sb("xm_ln", [128, GB, D])
        sq_ln = sb("sq_ln", [128, GB, D])
        sum_ln = sb("sum_ln", [128, GB])
        mean_ln = sb("mean_ln", [128, GB])
        var_ln = sb("var_ln", [128, GB])
        std_ln = sb("std_ln", [128, GB])
        rstd_ln = sb("rstd_ln", [128, GB])
        xs = sb("xs", [128, GB, 2, D])

        with ExitStack() as early:
            xring = sb("xring", [128, 3, NPATCH, QS * V], into=early)
            wg = sb("wg", [GF, D, C], into=early)
        x1t_hi = sb("x1t_hi", [128, NC, B, CH], f32r)
        x1t_lo = sb("x1t_lo", [128, NC, B, CH], f32r)

        with ExitStack() as att:
            h_t = sb("h_t", [128, B, NTOK], into=att)
            q_stack = sb("q_stack", [128, HEADS * D], f32r, into=att)
            e_t = sb("e_t", [128, HP, D], into=att)
            s_f = sb("s_f", [128, 2, GB, CH], into=att)
            s_hi = sb("s_hi", [128, 2, GB, CH], f32r, into=att)
            s_lo = sb("s_lo", [128, 2, GB, CH], f32r, into=att)
            s_tok = sb("s_tok", [128, 2, GB, D], into=att)
            with ExitStack() as prep:
                a_w = sb("a_w", [128, 2, QS, D], into=prep)
                a_pad = sb("a_pad", [128, D], into=prep)
                dft_sb = sb("dft_sb", [GF, 2, 2 * QS], into=prep)
                x_edge = sb("x_edge", [128, B, V], into=prep)
                nat = sb("nat", [128, HEADS * D], into=prep)
                nat2 = sb("nat2", [128, HEADS * D], into=prep)
                split_hi = sb("split_hi", [128, HEADS * D], f32r, into=prep)
                e_nat = sb("e_nat", [D, HP, 2 * D], into=prep)
            q_hi = sb("q_hi", [128, 2, HP, GB, CH], f32r, into=att)
            q_lo = sb("q_lo", [128, 2, HP, GB, CH], f32r, into=att)
            o_sb = sb("o_sb", [128, 2, 2, HP, CH], into=att)
            w_t = sb("w_t", [128, 2, HP, CH], into=att)
            g_sum = sb("g_sum", [128, B, D], into=att)
            g_hi = sb("g_hi", [128, B, 128], f32r, into=att)
            g_lo = sb("g_lo", [128, B, 128], f32r, into=att)

        with ExitStack() as ffn:
            w_bc = sb("w_bc", [128, EP, NTOK], into=ffn)
            feat = sb("feat", [128, NC, D], into=ffn)
            feat_t = sb("feat_t", [D, NTOK], into=ffn)
            logit = sb("logit", [128, NC, EXP], into=ffn)
            gate = sb("gate", [128, NC, EXP], into=ffn)
            red = sb("red", [128, 3, NC], into=ffn)
            gate_t = sb("gate_t", [EXP, NTOK], into=ffn)
            wbo = sb("wbo", [128, NC, D], into=ffn)
            h1 = sb("h1", [128, 2, EP, GT], into=ffn)
            h2r = sb("h2r", [128, 2, GT], into=ffn)
            h2w = sb("h2w", [128, 2, EP, GT], into=ffn)
            o_ln = sb("o_ln", [128, 2, GB, D], into=ffn)

        bank = [ctx.enter_context(nc.psum_tensor(f"bank{i}", [128, 512], f32)) for i in range(8)]

        x_loaded = [sem(f"x_loaded{i}") for i in range(3)]
        edge_loaded, wg_loaded, dft_loaded = sem("edge_loaded"), sem("wg_loaded"), sem("dft_loaded")
        const_loaded, q_loaded, e_loaded, w1_loaded = (sem("const_loaded"), sem("q_loaded"), sem("e_loaded"),
                                                       sem("w1_loaded"))
        par_loaded, w2_loaded, small_loaded = sem("par_loaded"), sem("w2_loaded"), sem("small_loaded")
        stored = [sem(f"stored{i}") for i in range(2)]
        w2_zeroed, fills, g_zeroed = sem("w2_zeroed"), sem("fills"), sem("g_zeroed")
        a_mm, a_ready, e_t_mm, e_t_ready, par_mm, par_ready = (sem("a_mm"), sem("a_ready"), sem("e_t_mm"),
                                                             sem("e_t_ready"), sem("par_mm"), sem("par_ready"))
        qs_hi_done, qs_top_done, qs_ready = sem("qs_hi_done"), sem("qs_top_done"), sem("qs_ready")
        ws_hi_done, ws_ready, bn_step, bn_sqrt, bn_ready = (sem("ws_hi_done"), sem("ws_ready"), sem("bn_step"),
                                                            sem("bn_sqrt"), sem("bn_ready"))
        tok_mm, ht_act, ht_dve = sem("tok_mm"), sem("ht_act"), sem("ht_dve")
        sf_done, sh_done, sl_done = sem("sf_done"), sem("sh_done"), sem("sl_done")
        q_mm, qh_done, ql_done = sem("q_mm"), sem("qh_done"), sem("ql_done")
        st_mm, st_done = sem("st_mm"), sem("st_done")
        score_mm, o_done, w_mm, wt_done, e_mm = (sem("score_mm"), sem("o_done"), sem("w_mm"), sem("wt_done"),
                                                 sem("e_mm"))
        g_mm, gsum_done, gh_done, gl_done = sem("g_mm"), sem("gsum_done"), sem("gh_done"), sem("gl_done")
        ln_y, ln_sum, ln_mean, ln_xm, ln_sq, ln_var, ln_std, ln_rstd = [
            sem(n) for n in ("ln_y", "ln_sum", "ln_mean", "ln_xm", "ln_sq", "ln_var", "ln_std", "ln_rstd")]
        xs_done, x1_done, feat_done = sem("xs_done"), sem("x1_done"), sem("feat_done")
        xt_mm, xth_done, xtl_done = sem("xt_mm"), sem("xth_done"), sem("xtl_done")
        feat_sum, ft_mm, ft_done, lg_mm, soft, gate_exp = (sem("feat_sum"), sem("ft_mm"), sem("ft_done"),
                                                           sem("lg_mm"), sem("soft"), sem("gate_exp"))
        gt_mm, gt_done, wb_mm, wb_done, wbo_mm, wbo_done, x1b_done = (
            sem("gt_mm"), sem("gt_done"), sem("wb_mm"), sem("wb_done"), sem("wbo_mm"), sem("wbo_done"),
            sem("x1b_done"))
        z1_mm, h1_done, z2_mm, h2r_done, h2w_done, f3_mm = (sem("z1_mm"), sem("h1_done"), sem("z2_mm"),
                                                            sem("h2r_done"), sem("h2w_done"), sem("f3_mm"))
        o_y, o_sum, o_mean, o_xm, o_sq, o_var, o_std, o_rstd, o_ready = [
            sem(n) for n in ("o_y", "o_sum", "o_mean", "o_xm", "o_sq", "o_var", "o_std", "o_rstd", "o_ready")]

        def group(ap, bh, c):
            return ap[:, bass.ds(c, 1), GB * bh:GB * bh + GB, :].rearrange("p a b n -> p (a b) n")

        def over_batch(ap, n):
            return ap.unsqueeze(1).broadcast_to((128, GB, n))

        def per_token(ap):
            return ap.unsqueeze(2).broadcast_to((128, GB, D))

        def bank3(i, a):
            return bank[i][:, :].rearrange("p (a b) -> p a b", a=a)

        slots = [xring[:, s, :, :].rearrange("p m (s v) -> p m s v", s=QS) for s in range(3)]
        score_bank, qt_bank, w_bank, e_bank, g_bank = (0, 1, 2, 3), 4, 5, 6, 7
        z1_bank, z2_bank, y_bank = (0, 1), (2, 3), (4, 5)

        block = ctx.enter_context(nc.Block())

        @block.sync
        def _(sp):
            with nc.allow_non_contiguous_dma(reason="64-channel rows of the tokenizer weight"):
                sp.dma_start(wg[:, :, :], tok_w.rearrange("o (g c) -> g o c", c=C)).then_inc(wg_loaded, 16)
            sp.dma_start(dft_sb[:, :, :], dft).then_inc(dft_loaded, 16)

            def load_x(b):
                if b >= 3:
                    sp.wait_ge(tok_mm, 4 * ((b - 3) // 2 + 1))
                src = x[b].rearrange("c (m h s) v -> h c m (s v)", h=2, s=QS)
                for half in range(2):
                    sp.dma_start(xring[64 * half:64 * half + 64, b % 3, :, :], src[half]).then_inc(x_loaded[b % 3], 16)

            load_x(0)
            for half in range(2):
                sp.dma_start(x_edge[64 * half:64 * half + 64, :, :],
                             x[:, :, T - 1, :].rearrange("b c v -> c b v")).then_inc(edge_loaded, 16)
            for b in range(1, B):
                load_x(b)

            out_v = out.rearrange("b (c p) d -> p c b d", p=CH)

            def store(m, c, bh):
                sp.wait_ge(o_ready, m + 1)
                sp.dma_start(group(out_v, bh, c), o_ln[:, bh, :, :]).then_inc(stored[bh], 16)

            with sp.Fori(0, NC) as c:
                for bh in range(2):
                    store(2 * c + bh, c, bh)
            for bh in range(2):
                sp.wait_ge(stored[bh], 16 * NC)

        @block.gpsimd
        def _(pool):
            nc.gpsimd.memset(w2_diag[:, :, :], 0.0).then_inc(w2_zeroed, 1)
            nc.gpsimd.memset(ones_row[:, :], 1.0).then_inc(fills, 1)
            nc.gpsimd.memset(eps_ln[:, :], LN_EPS).then_inc(fills, 1)
            nc.gpsimd.memset(eps_bn[:, :], BN_EPS).then_inc(fills, 1)
            nc.gpsimd.memset(g_sum[:, :, :], 0.0).then_inc(g_zeroed, 1)
            for g in (g_hi, g_lo):
                nc.gpsimd.memset(g[:, :, :].bitcast(f32), 0.0).then_inc(g_zeroed, 1)
            pool.wait_ge(g_zeroed, 3)

            def s_low(m, bh, after_g):
                pool.wait_ge(sh_done, m + 1)
                if after_g:
                    pool.wait_ge(gl_done, 2 * m - 4)
                nc.gpsimd.tensor_tensor(s_lo[:, bh, :, :], s_f[:, bh, :, :], s_hi[:, bh, :, :],
                                        ALU.subtract).then_inc(sl_done, 1)

            def g_low(m, bh):
                bs = slice(GB * bh, GB * bh + GB)
                for h2 in range(2):
                    rows, cols = slice(64 * h2, 64 * h2 + 64), slice(64 * h2, 64 * h2 + 64)
                    pool.wait_ge(gh_done, 2 * m + 1 + h2)
                    if h2:
                        pool.wait_ge(gl_done, 2 * m + 1)
                    else:
                        pool.wait_ge(sl_done, m + 2)
                    nc.gpsimd.tensor_tensor(g_lo[rows, bs, cols], g_sum[rows, bs, :], g_hi[rows, bs, cols],
                                            ALU.subtract).then_inc(gl_done, 1)

            def step(c, bh, kind):
                m = 2 * c + bh
                if not (kind == "first" and bh == 0) and not (kind == "last" and bh == 1):
                    g_low(m - 1, 1 - bh)
                if kind != "last":
                    s_low(m + 2, bh, not (kind == "first" and bh == 0))

            s_low(0, 0, False)
            s_low(1, 1, False)
            for bh in range(2):
                step(0, bh, "first")
            with pool.Fori(1, NC - 1) as c:
                for bh in range(2):
                    step(c, bh, "mid")
            for bh in range(2):
                step(NC - 1, bh, "last")

            pool.wait_ge(wbo_done, 1)
            pool.wait_ge(x1_done, NG)
            for c in range(NC):
                nc.gpsimd.tensor_tensor(x1[:, c, :, :], x1[:, c, :, :],
                                        wbo[:, c, :].unsqueeze(1).broadcast_to((128, B, D)),
                                        ALU.add).then_inc(x1b_done, 1)

        @block.scalar
        def _(act):
            act.dma_start(ident[:, :], ident_in).then_inc(const_loaded, 16)
            act.dma_start(mask[:, :], mask_in).then_inc(const_loaded, 16)
            for h2 in range(2):
                src = att_e[HP * h2:HP * h2 + HP].rearrange("hp i j -> i hp j")
                act.dma_start(e_nat[:, :, D * h2:D * h2 + D], src).then_inc(e_loaded, 16)
            nat_v = nat[:, :].rearrange("p (hp h2 j) -> p hp h2 j", hp=HP, h2=2)
            for half in range(2):
                rows = slice(64 * half, 64 * half + 64)
                for h2 in range(2):
                    act.dma_start(nat_v[rows, :, h2, :],
                                  att_q[HP * h2:HP * h2 + HP].rearrange("hp i j -> i hp j")).then_inc(q_loaded, 16)
                act.dma_start(nat2[rows, :].rearrange("p (e h) -> p e h", e=EXP),
                              w1.rearrange("e d h -> d e h")).then_inc(w1_loaded, 16)
            for n, p in enumerate((b1, g1, be1, m1, v1, b2, g2, be2, m2, v2)):
                act.dma_start(par_rows[EP * n:EP * n + EP, :],
                              p.rearrange("(ep e2) h -> ep (e2 h)", e2=2)).then_inc(par_loaded, 16)
            act.wait_ge(w2_zeroed, 1)
            w2_v = w2.rearrange("(ep e2) h k -> e2 h ep k", e2=2)
            for e2 in range(2):
                blk = slice(64 * e2, 64 * e2 + 64)
                act.dma_start(w2_diag[blk, :, blk], w2_v[e2]).then_inc(w2_loaded, 16)
            act.dma_start(wo_pair[:, :, :], wo.rearrange("(ep e2) h d -> (e2 h) ep d", e2=2)).then_inc(small_loaded, 16)
            act.dma_start(wr_sb[:, :], wr).then_inc(small_loaded, 16)
            act.dma_start(br_sb[:, :], br.rearrange("(a e) -> a e", a=1)).then_inc(small_loaded, 16)
            act.dma_start(bo_sb[:, :], bo).then_inc(small_loaded, 16)
            act.dma_start(sel_sb[:, :], sel_in).then_inc(small_loaded, 16)

            act.wait_ge(q_loaded, 64)
            nc.scalar.activation(split_hi[:, :], nat[:, :], ACT.Copy).then_inc(qs_hi_done, 1)
            nc.scalar.activation(q_stack[0:64, :], nat[0:64, :], ACT.Copy).then_inc(qs_top_done, 1)
            act.wait_ge(w1_loaded, 32)
            act.wait_ge(qs_ready, 1)
            nc.scalar.activation(split_hi[:, :], nat2[:, :], ACT.Copy).then_inc(ws_hi_done, 1)
            nc.scalar.activation(w1_stack[0:64, :], nat2[0:64, :], ACT.Copy).then_inc(ws_hi_done, 1)
            act.wait_ge(par_ready, 1)
            act.wait_ge(fills, 3)
            for n in range(2):
                nc.scalar.activation(bn_tmp[:, n, :], par[:, 5 * n + 4, :], ACT.Sqrt, bias=eps_bn[:, :]).then_inc(bn_sqrt, 1)

            hv = h_t[:, :, :].rearrange("p b (v n) -> p b n v", n=NPATCH)
            for p in range(B // 2):
                for g in range(2):
                    act.wait_ge(tok_mm, 4 * p + 2 * g + 2)
                    src = bank3(2 * (p % 2) + g, 8)[0:64]
                    for half in range(2):
                        nc.scalar.activation(hv[64 * half:64 * half + 64, 2 * p, 8 * g:8 * g + 8, :], src,
                                             ACT.Copy).then_inc(ht_act, 1)

            def s_high(m, bh, free):
                act.wait_ge(sf_done, m + 1)
                if free:
                    act.wait_ge(score_mm, 8 * m - 8)
                    act.wait_ge(sl_done, m - 1)
                nc.scalar.activation(s_hi[:, bh, :, :], s_f[:, bh, :, :], ACT.Copy).then_inc(sh_done, 1)

            def q_high(m, bh, hp, free):
                act.wait_ge(q_mm, 4 * m + hp + 1)
                if free and hp == 0:
                    act.wait_ge(w_mm, 4 * m - 4)
                nc.scalar.activation(q_hi[:, bh, hp, :, :], bank3(qt_bank, GB), ACT.Copy).then_inc(qh_done, 1)

            def s_tokens(m, bh, free):
                act.wait_ge(st_mm, m + 1)
                if free:
                    act.wait_ge(w_mm, 4 * m - 4)
                    act.wait_ge(g_mm, m - 1)
                    act.wait_ge(ln_y, m - 1)
                nc.scalar.activation(s_tok[:, bh, :, :],
                                     bank[qt_bank][:, 0:GB * D].rearrange("p (a b) -> p a b", a=GB),
                                     ACT.Copy).then_inc(st_done, 1)

            def w_copy(k, par_k, free):
                act.wait_ge(w_mm, k + 1)
                if free:
                    act.wait_ge(e_mm, k - 1)
                nc.scalar.activation(w_t[:, par_k, :, :], bank3(w_bank, HP), ACT.Copy).then_inc(wt_done, 1)

            def keep_x1(m, c, bh):
                act.wait_ge(xs_done, m + 1)
                nc.scalar.activation(group(x1, bh, c), xs[:, :, 0, :], ACT.Copy).then_inc(x1_done, 1)

            def g_high(m, bh):
                act.wait_ge(gsum_done, m + 1)
                act.wait_ge(w_mm, 4 * m + 4)
                bs = slice(GB * bh, GB * bh + GB)
                for h2 in range(2):
                    blk = slice(64 * h2, 64 * h2 + 64)
                    nc.scalar.activation(g_hi[blk, bs, blk], g_sum[blk, bs, :], ACT.Copy).then_inc(gh_done, 1)

            def x_high(m, c, bh):
                act.wait_ge(xt_mm, m + 1)
                nc.scalar.activation(group(x1t_hi, bh, c), bank3(qt_bank, GB), ACT.Copy).then_inc(xth_done, 1)

            def ln_square(m, s_xm, s_sq):
                act.wait_ge(s_xm, m + 1)
                nc.scalar.activation(sq_ln[:, :, :], xm_ln[:, :, :], ACT.Square).then_inc(s_sq, 1)

            def ln_sqrt(m, s_var, s_std):
                act.wait_ge(s_var, m + 1)
                nc.scalar.activation(std_ln[:, :], var_ln[:, :], ACT.Sqrt, bias=eps_ln[:, :],
                                     scale=1.0 / D).then_inc(s_std, 1)

            def step(c, bh, kind):
                m = 2 * c + bh
                prev = not (kind == "first" and bh == 0)
                ahead = not (kind == "last" and bh == 1)
                for u in range(GB):
                    k = 4 * m + u
                    if ahead and u < 2:
                        q_high(m + 1, 1 - bh, 2 * u, prev)
                    w_copy(k, u % 2, prev or u >= 2)
                    if ahead and u < 2:
                        q_high(m + 1, 1 - bh, 2 * u + 1, prev)
                    if prev and u == 0:
                        ln_square(m - 1, ln_xm, ln_sq)
                    if prev and u == 1:
                        ln_sqrt(m - 1, ln_var, ln_std)
                        if ahead:
                            g_high(m - 1, 1 - bh)
                    if ahead and u == 2:
                        s_tokens(m + 1, 1 - bh, prev)
                    if kind != "last" and u == 2:
                        s_high(m + 2, bh, True)
                    if prev and u == 3:
                        keep_x1(m - 1, c if bh else c - 1, 1 - bh)
                        x_high(m - 1, c if bh else c - 1, 1 - bh)

            act.wait_ge(g_zeroed, 3)
            s_high(0, 0, False)
            for hp in range(HP):
                q_high(0, 0, hp, False)
            s_tokens(0, 0, False)
            s_high(1, 1, False)
            for bh in range(2):
                step(0, bh, "first")
            with act.Fori(1, NC - 1) as c:
                for bh in range(2):
                    step(c, bh, "mid")
            for bh in range(2):
                step(NC - 1, bh, "last")
            ln_square(NG - 1, ln_xm, ln_sq)
            ln_sqrt(NG - 1, ln_var, ln_std)
            keep_x1(NG - 1, NC - 1, 1)
            x_high(NG - 1, NC - 1, 1)

            for i in range(2):
                act.wait_ge(ft_mm, 4 * i + 4)
                nc.scalar.activation(feat_t[:, GT * i:GT * i + GT], bank[i][0:D, :], ACT.Copy,
                                     scale=1.0 / B).then_inc(ft_done, 1)
            act.wait_ge(soft, 3)
            nc.scalar.activation(gate[:, :, :], logit[:, :, :], ACT.Exp).then_inc(gate_exp, 1)
            for i in range(2):
                act.wait_ge(gt_mm, 4 * i + 4)
                nc.scalar.activation(gate_t[:, GT * i:GT * i + GT], bank[3 + i][0:EXP, :], ACT.Copy).then_inc(gt_done, 1)
            for i in range(2 * EP):
                act.wait_ge(wb_mm, i + 1)
                nc.scalar.activation(w_bc[:, i % EP, GT * (i // EP):GT * (i // EP) + GT], bank[i % 2][:, :],
                                     ACT.Copy).then_inc(wb_done, 1)
            act.wait_ge(wbo_mm, NC)
            nc.scalar.activation(wbo[:, :, :], bank3(5, NC), ACT.Copy).then_inc(wbo_done, 1)

            def hidden1(m, bh, ep, free):
                act.wait_ge(z1_mm, 4 * m + ep + 1)
                if free and ep == 0:
                    act.wait_ge(z2_mm, 4 * m - 4)
                nc.scalar.activation(h1[:, bh, ep, :], bank[z1_bank[ep % 2]][:, :], ACT.Relu,
                                     bias=bn_bias[:, 0, ep:ep + 1], scale=bn_scale[:, 0, ep:ep + 1]).then_inc(h1_done, 1)

            def hidden2(m, ep, free):
                act.wait_ge(z2_mm, 4 * m + ep + 1)
                if free or ep >= 2:
                    act.wait_ge(h2w_done, 4 * m + ep - 1)
                nc.scalar.activation(h2r[:, ep % 2, :], bank[z2_bank[ep % 2]][:, :], ACT.Relu,
                                     bias=bn_bias[:, 1, ep:ep + 1], scale=bn_scale[:, 1, ep:ep + 1]).then_inc(h2r_done, 1)

            def expert_step(c, bh, kind):
                m = 2 * c + bh
                for ep in range(EP):
                    if not (kind == "last" and bh == 1):
                        hidden1(m + 1, 1 - bh, ep, not (kind == "first" and bh == 0))
                    hidden2(m, ep, not (kind == "first" and bh == 0))
                    if not kind == "first":
                        if ep == 1:
                            ln_square(m - 2, o_xm, o_sq)
                        if ep == 3:
                            ln_sqrt(m - 2, o_var, o_std)

            act.wait_ge(bn_ready, 2)
            for ep in range(EP):
                hidden1(0, 0, ep, False)
            for bh in range(2):
                expert_step(0, bh, "first")
            with act.Fori(1, NC - 1) as c:
                for bh in range(2):
                    expert_step(c, bh, "mid")
            for bh in range(2):
                expert_step(NC - 1, bh, "last")
            for m in (NG - 2, NG - 1):
                ln_square(m, o_xm, o_sq)
                ln_sqrt(m, o_var, o_std)

        @block.vector
        def _(dve):
            dve.wait_ge(a_mm, 2)
            psa = bank[4][:, :].rearrange("p (o k) -> p k o", k=2 * QS)
            nc.vector.tensor_copy(a_w[:, :, :, :].rearrange("p q s o -> p (q s) o"), psa).then_inc(a_ready, 1)
            nc.vector.tensor_reduce(a_pad[:, :], bank[4][:, :].rearrange("p (o k) -> p o k", k=2 * QS)[:, :, QS:2 * QS],
                                    AX.X, ALU.add).then_inc(a_ready, 1)
            dve.wait_ge(e_t_mm, 1)
            nc.vector.tensor_copy(e_t[:, :, :], bank[6][:, 0:HP * D].rearrange("p (a b) -> p a b", a=HP)).then_inc(e_t_ready, 1)
            dve.wait_ge(par_mm, 1)
            nc.vector.tensor_copy(par[:, :, :].rearrange("p n e -> p (n e)"), bank[5][:, 0:NPAR * EP]).then_inc(par_ready, 1)
            dve.wait_ge(q_loaded, 64)
            dve.wait_ge(qs_hi_done, 1)
            nc.vector.tensor_tensor(q_stack[64:128, :], nat[64:128, :], split_hi[64:128, :], ALU.subtract).then_inc(qs_ready, 1)
            dve.wait_ge(w1_loaded, 32)
            dve.wait_ge(ws_hi_done, 1)
            nc.vector.tensor_tensor(w1_stack[64:128, :], nat2[64:128, :], split_hi[64:128, :], ALU.subtract).then_inc(ws_ready, 1)
            dve.wait_ge(bn_sqrt, 2)
            dve.wait_ge(par_ready, 1)
            nc.vector.reciprocal(bn_scale[:, :, :], bn_tmp[:, :, :]).then_inc(bn_step, 1)
            for n in range(2):
                dve.wait_ge(bn_step, 4 * n + 1)
                nc.vector.tensor_tensor(bn_scale[:, n, :], bn_scale[:, n, :], par[:, 5 * n + 1, :], ALU.mult).then_inc(bn_step, 1)
                nc.vector.tensor_tensor(bn_bias[:, n, :], par[:, 5 * n, :], par[:, 5 * n + 3, :], ALU.subtract).then_inc(bn_step, 1)
                dve.wait_ge(bn_step, 4 * n + 3)
                nc.vector.tensor_tensor(bn_bias[:, n, :], bn_bias[:, n, :], bn_scale[:, n, :], ALU.mult).then_inc(bn_step, 1)
                dve.wait_ge(bn_step, 4 * n + 4)
                nc.vector.tensor_tensor(bn_bias[:, n, :], bn_bias[:, n, :], par[:, 5 * n + 2, :], ALU.add).then_inc(bn_step, 1)
            dve.wait_ge(bn_step, 9)
            nc.vector.tensor_copy(bn_tmp[:, 0, :], bn_bias[:, 0, :]).then_inc(bn_ready, 2)

            hv = h_t[:, :, :].rearrange("p b (v n) -> p b n v", n=NPATCH)
            for p in range(B // 2):
                for g in range(2):
                    dve.wait_ge(tok_mm, 4 * p + 2 * g + 2)
                    src = bank3(2 * (p % 2) + g, 8)[64:128]
                    for half in range(2):
                        nc.vector.tensor_copy(hv[64 * half:64 * half + 64, 2 * p + 1, 8 * g:8 * g + 8, :],
                                              src).then_inc(ht_dve, 1)

            def s_stage(m, c, bh, free):
                if free:
                    dve.wait_ge(st_mm, m - 1)
                    dve.wait_ge(sl_done, m - 1)
                nc.vector.tensor_copy(s_f[:, bh, :, :],
                                      h_t[:, GB * bh:GB * bh + GB, bass.ds(c * CH, CH)]).then_inc(sf_done, 1)

            def q_low(m, bh, hp):
                dve.wait_ge(qh_done, 4 * m + hp + 1)
                nc.vector.tensor_tensor(q_lo[:, bh, hp, :, :], bank3(qt_bank, GB), q_hi[:, bh, hp, :, :],
                                        ALU.subtract).then_inc(ql_done, 1)

            def mask_scores(k, par_k, free):
                if free:
                    dve.wait_ge(w_mm, k - 1)
                for h2 in range(2):
                    dve.wait_ge(score_mm, 2 * k + h2 + 1)
                    nc.vector.tensor_tensor(o_sb[:, par_k, h2, :, :], bank3(score_bank[2 * par_k + h2], HP),
                                            mask[:, :].unsqueeze(1).broadcast_to((128, HP, CH)),
                                            ALU.mult).then_inc(o_done, 1)

            def ln_first(m, s):
                dve.wait_ge(s["y"], m + 1)
                nc.vector.tensor_reduce(sum_ln[:, :], y_ln[:, :, :], AX.X, ALU.add).then_inc(s["sum"], 1)
                dve.wait_ge(s["sum"], m + 1)
                nc.vector.tensor_scalar(mean_ln[:, :], sum_ln[:, :], 1.0 / D, None, ALU.mult).then_inc(s["mean"], 1)
                dve.wait_ge(s["mean"], m + 1)
                nc.vector.tensor_tensor(xm_ln[:, :, :], y_ln[:, :, :], per_token(mean_ln[:, :]),
                                        ALU.subtract).then_inc(s["xm"], 1)

            def ln_var_sum(m, s):
                dve.wait_ge(s["sq"], m + 1)
                nc.vector.tensor_reduce(var_ln[:, :], sq_ln[:, :, :], AX.X, ALU.add).then_inc(s["var"], 1)

            def ln_scale(m, s, dst, done):
                dve.wait_ge(s["std"], m + 1)
                nc.vector.reciprocal(rstd_ln[:, :], std_ln[:, :]).then_inc(s["rstd"], 1)
                dve.wait_ge(s["rstd"], m + 1)
                if dst is xs:
                    nc.vector.tensor_tensor(xs[:, :, :, :], xm_ln[:, :, :].unsqueeze(2).broadcast_to((128, GB, 2, D)),
                                            rstd_ln[:, :].unsqueeze(2).unsqueeze(3).broadcast_to((128, GB, 2, D)),
                                            ALU.mult).then_inc(done, 1)
                else:
                    nc.vector.tensor_tensor(dst, xm_ln[:, :, :], per_token(rstd_ln[:, :]), ALU.mult).then_inc(done, 1)

            ln1 = dict(y=ln_y, sum=ln_sum, mean=ln_mean, xm=ln_xm, sq=ln_sq, var=ln_var, std=ln_std, rstd=ln_rstd)
            ln2 = dict(y=o_y, sum=o_sum, mean=o_mean, xm=o_xm, sq=o_sq, var=o_var, std=o_std, rstd=o_rstd)

            def residual(m, bh):
                dve.wait_ge(e_mm, 4 * m + 4)
                nc.vector.tensor_tensor(y_ln[:, :, :], bank[e_bank][:, 0:GB * D].rearrange("p (a b) -> p a b", a=GB),
                                        s_tok[:, bh, :, :], ALU.add).then_inc(ln_y, 1)

            def g_add(m, bh):
                dve.wait_ge(g_mm, m + 1)
                bs = slice(GB * bh, GB * bh + GB)
                nc.vector.tensor_tensor(g_sum[:, bs, :], g_sum[:, bs, :],
                                        bank[g_bank][:, 0:GB * D].rearrange("p (a b) -> p a b", a=GB),
                                        ALU.add).then_inc(gsum_done, 1)

            def finish_x1(m, free):
                if free:
                    dve.wait_ge(x1_done, m)
                    dve.wait_ge(xt_mm, m)
                ln_scale(m, ln1, xs, xs_done)
                dve.wait_ge(xs_done, m + 1)
                nc.vector.tensor_reduce(feat_half[:, bass.ds(m, 1), :].rearrange("p a d -> p (a d)"),
                                        xs[:, :, 0, :].rearrange("p b d -> p d b"), AX.X, ALU.add).then_inc(feat_done, 1)

            def x_low(m, c, bh):
                dve.wait_ge(xth_done, m + 1)
                nc.vector.tensor_tensor(group(x1t_lo, bh, c), bank3(qt_bank, GB), group(x1t_hi, bh, c),
                                        ALU.subtract).then_inc(xtl_done, 1)

            def step(c, bh, kind):
                m = 2 * c + bh
                prev = not (kind == "first" and bh == 0)
                ahead = not (kind == "last" and bh == 1)
                for u in range(GB):
                    k = 4 * m + u
                    if ahead or u < GB - 1:
                        mask_scores(k + 1, (u + 1) % 2, prev or u >= 1)
                    if ahead and u < 2:
                        q_low(m + 1, 1 - bh, 2 * u)
                    if prev:
                        if u == 0:
                            residual(m - 1, 1 - bh)
                            if ahead:
                                if kind != "first":
                                    dve.wait_ge(gl_done, 2 * m - 2)
                                g_add(m - 1, 1 - bh)
                            ln_first(m - 1, ln1)
                        if u == 1:
                            ln_var_sum(m - 1, ln1)
                        if u == 2:
                            finish_x1(m - 1, not (kind == "first" and bh == 1))
                    if ahead and u < 2:
                        q_low(m + 1, 1 - bh, 2 * u + 1)
                    if kind != "last" and u == 2:
                        s_stage(m + 2, c + 1, bh, True)
                    if prev and u == 3:
                        x_low(m - 1, c if bh else c - 1, 1 - bh)

            dve.wait_ge(ht_dve, 2 * B)
            dve.wait_ge(ht_act, 2 * B)
            s_stage(0, 0, 0, False)
            s_stage(1, 0, 1, False)
            dve.wait_ge(const_loaded, 32)
            for hp in range(HP):
                q_low(0, 0, hp)
            mask_scores(0, 0, False)
            for bh in range(2):
                step(0, bh, "first")
            with dve.Fori(1, NC - 1) as c:
                for bh in range(2):
                    step(c, bh, "mid")
            for bh in range(2):
                step(NC - 1, bh, "last")
            residual(NG - 1, 1)
            ln_first(NG - 1, ln1)
            ln_var_sum(NG - 1, ln1)
            finish_x1(NG - 1, True)

            dve.wait_ge(feat_done, NG)
            fh = feat_half[:, :, :].rearrange("p (c b) d -> p c b d", b=2)
            nc.vector.tensor_tensor(feat[:, :, :], fh[:, :, 0, :], fh[:, :, 1, :], ALU.add).then_inc(feat_sum, 1)
            x_low(NG - 1, NC - 1, 1)
            dve.wait_ge(lg_mm, NC)
            ps_lg = bank[2][:, 0:NC * EXP].rearrange("p (c e) -> p c e", e=EXP)
            nc.vector.tensor_copy(logit[:, :, :], ps_lg).then_inc(soft, 1)
            dve.wait_ge(soft, 1)
            nc.vector.tensor_reduce(red[:, 0, :], logit[:, :, :], AX.X, ALU.max).then_inc(soft, 1)
            dve.wait_ge(soft, 2)
            nc.vector.tensor_tensor(logit[:, :, :], logit[:, :, :],
                                    red[:, 0, :].unsqueeze(2).broadcast_to((128, NC, EXP)), ALU.subtract).then_inc(soft, 1)
            dve.wait_ge(gate_exp, 1)
            nc.vector.tensor_reduce(red[:, 1, :], gate[:, :, :], AX.X, ALU.add).then_inc(soft, 1)
            dve.wait_ge(soft, 4)
            nc.vector.reciprocal(red[:, 2, :], red[:, 1, :]).then_inc(soft, 1)
            dve.wait_ge(soft, 5)
            nc.vector.tensor_tensor(gate[:, :, :], gate[:, :, :],
                                    red[:, 2, :].unsqueeze(2).broadcast_to((128, NC, EXP)), ALU.mult).then_inc(soft, 1)

            def gate_hidden(m, c, bh, ep, free):
                dve.wait_ge(h2r_done, 4 * m + ep + 1)
                if free and ep == 0:
                    dve.wait_ge(f3_mm, 4 * m - 4)
                nc.vector.tensor_tensor(
                    h2w[:, bh, ep, :].rearrange("p (b t) -> p b t", b=GB),
                    h2r[:, ep % 2, :].rearrange("p (b t) -> p b t", b=GB),
                    w_bc[:, ep, bass.ds(c * CH, CH)].unsqueeze(1).broadcast_to((128, GB, CH)),
                    ALU.mult).then_inc(h2w_done, 1)

            def out_residual(m, c, bh):
                dve.wait_ge(f3_mm, 4 * m + 4)
                nc.vector.tensor_tensor(y_ln[:, :, :],
                                        bank[y_bank[bh]][:, 0:GB * D].rearrange("p (a b) -> p a b", a=GB),
                                        group(x1, bh, c), ALU.add).then_inc(o_y, 1)

            def out_scale(m, c, bh, free):
                if free:
                    dve.wait_ge(stored[bh], 16 * c)
                ln_scale(m, ln2, o_ln[:, bh, :, :], o_ready)

            def expert_step(c, bh, kind):
                m = 2 * c + bh
                late = kind != "first"
                for ep in range(EP):
                    gate_hidden(m, c, bh, ep, late)
                    if late:
                        if ep == 0:
                            out_residual(m - 2, c - 1, bh)
                            ln_first(m - 2, ln2)
                        if ep == 2:
                            ln_var_sum(m - 2, ln2)
                if late:
                    out_scale(m - 2, c - 1, bh, kind != "second")

            dve.wait_ge(wb_done, 2 * EP)
            dve.wait_ge(x1b_done, NC)
            for bh in range(2):
                expert_step(0, bh, "first")
            for bh in range(2):
                expert_step(1, bh, "second")
            with dve.Fori(2, NC) as c:
                for bh in range(2):
                    expert_step(c, bh, "mid")
            for m in (NG - 2, NG - 1):
                out_residual(m, NC - 1, m % 2)
                ln_first(m, ln2)
                ln_var_sum(m, ln2)
                out_scale(m, NC - 1, m % 2, True)

        @block.tensor
        def _(pe):
            def mm(o, lhs_t, rhs, start=True, stop=True):
                return nc.tensor.matmul(o, lhs_t, rhs, start=start, stop=stop, skip_group_check=True)

            pe.wait_ge(wg_loaded, 16)
            pe.wait_ge(dft_loaded, 16)
            for o in range(D):
                for half in range(2):
                    last = mm(bank[4][64 * half:64 * half + 64, 2 * QS * o:2 * QS * (o + 1)], wg[:, o, :],
                              dft_sb[:, half, :])
                    if o == D - 1:
                        last.then_inc(a_mm, 1)
            pe.wait_ge(const_loaded, 32)
            pe.wait_ge(e_loaded, 32)
            for hp in range(HP):
                last = nc.tensor.transpose(bank[6][:, D * hp:D * hp + D], e_nat[:, hp, :], ident[0:D, 0:D])
            last.then_inc(e_t_mm, 1)
            pe.wait_ge(par_loaded, 16 * NPAR)
            nc.tensor.transpose(bank[5][:, 0:NPAR * EP], par_rows[:, :], ident[0:NPAR * EP, 0:NPAR * EP]).then_inc(par_mm, 1)

            pe.wait_ge(a_ready, 2)
            for p in range(B // 2):
                for j in range(2):
                    b = 2 * p + j
                    pe.wait_ge(x_loaded[b % 3], 32 * (b // 3 + 1))
                for g in range(2):
                    if p >= 2:
                        pe.wait_ge(ht_act, 4 * (p - 2) + 2 * g + 2)
                        pe.wait_ge(ht_dve, 4 * (p - 2) + 2 * g + 2)
                    ps = bank3(2 * (p % 2) + g, 8)
                    for q in range(2):
                        n = 8 if q == 0 or g == 0 else 7
                        for s in range(QS):
                            for j in range(2):
                                b = 2 * p + j
                                last = mm(ps[64 * j:64 * j + 64, 0:n, :], a_w[:, q, s, :],
                                          slots[b % 3][:, 8 * g + q:8 * g + q + n, s, :], start=(q + s == 0),
                                          stop=(g == 0 and q == 1 and s == QS - 1))
                                if g == 0 and q == 1 and s == QS - 1:
                                    last.then_inc(tok_mm, 1)
                    if g == 1:
                        if p == 0:
                            pe.wait_ge(edge_loaded, 32)
                        for j in range(2):
                            mm(ps[64 * j:64 * j + 64, 7, :], a_pad[:, :], x_edge[:, 2 * p + j, :],
                               start=False).then_inc(tok_mm, 1)

            def queries(m, bh, hp):
                cols = slice(128 * hp, 128 * hp + 128)
                mm(bank[qt_bank][:, :], q_stack[:, cols], s_hi[:, bh, :, :], stop=False)
                mm(bank[qt_bank][:, :], q_stack[:, cols], s_lo[:, bh, :, :], start=False).then_inc(q_mm, 1)

            def transposes(bh):
                for u in range(GB):
                    last = nc.tensor.transpose(bank[qt_bank][:, D * u:D * u + D], s_f[0:D, bh, u, :], ident[0:D, 0:D])
                last.then_inc(st_mm, 1)

            def scores(k, bh, u, free):
                for h2 in range(2):
                    rows = slice(64 * h2, 64 * h2 + 64)
                    if free:
                        pe.wait_ge(o_done, 2 * k - 3 + h2)
                    o = bank[score_bank[2 * (u % 2) + h2]][:, :]
                    mm(o, s_hi[rows, bh, u, :], q_hi[rows, bh, :, u, :], stop=False)
                    mm(o, s_hi[rows, bh, u, :], q_lo[rows, bh, :, u, :], start=False, stop=False)
                    mm(o, s_lo[rows, bh, u, :], q_hi[rows, bh, :, u, :], start=False).then_inc(score_mm, 1)

            def values(m, k, bh, u, kind):
                if not (kind == "first" and bh == 0 and u == 0):
                    pe.wait_ge(wt_done, k)
                inter = kind != "first"
                if inter:
                    if u == 0:
                        pe.wait_ge(gl_done, 2 * m - 2)
                    b = GB * bh + u
                    mm(bank[w_bank][:, :], g_hi[:, b, :], q_hi[:, bh, :, u, :], stop=False)
                    mm(bank[w_bank][:, :], g_hi[:, b, :], q_lo[:, bh, :, u, :], start=False, stop=False)
                    mm(bank[w_bank][:, :], g_lo[:, b, :], q_hi[:, bh, :, u, :], start=False, stop=False)
                if u == 0:
                    pe.wait_ge(st_done, m + 1)
                for h2 in range(2):
                    pe.wait_ge(o_done, 2 * k + h2 + 1)
                    last = mm(bank[w_bank][64 * h2:64 * h2 + 64, :], s_tok[:, bh, u, :], o_sb[:, u % 2, h2, :, :],
                              start=not inter)
                last.then_inc(w_mm, 1)

            def state(m, bh, u, free):
                if u == 0 and free:
                    pe.wait_ge(gsum_done, m)
                for half in range(2):
                    last = mm(bank[g_bank][64 * half:64 * half + 64, D * u:D * u + D], s_tok[:, bh, u, :],
                              s_tok[:, bh, u, :])
                if u == GB - 1:
                    last.then_inc(g_mm, 1)

            def outputs(m, k, bh, u, free):
                if u == 0 and free:
                    pe.wait_ge(ln_y, m)
                pe.wait_ge(wt_done, k + 1)
                for hp in range(HP):
                    last = mm(bank[e_bank][:, D * u:D * u + D], w_t[:, u % 2, hp, :], e_t[:, hp, :],
                              start=(hp == 0), stop=(hp == HP - 1))
                last.then_inc(e_mm, 1)

            def x_transposes(m):
                pe.wait_ge(xs_done, m + 1)
                for u in range(GB):
                    last = nc.tensor.transpose(bank[qt_bank][:, CH * u:CH * u + CH],
                                               xs[:, u, :, :].rearrange("p r d -> p (r d)"), ident[:, :])
                last.then_inc(xt_mm, 1)

            def step(c, bh, kind):
                m = 2 * c + bh
                prev = not (kind == "first" and bh == 0)
                ahead = not (kind == "last" and bh == 1)
                for u in range(GB):
                    k = 4 * m + u
                    if ahead or u < GB - 1:
                        if u == GB - 1:
                            pe.wait_ge(ql_done, 4 * m + 8)
                        scores(k + 1, bh if u < GB - 1 else 1 - bh, (u + 1) % GB, prev or u >= 1)
                    if ahead and u < 2:
                        if u == 0:
                            pe.wait_ge(sl_done, m + 2)
                            if kind != "first":
                                pe.wait_ge(xtl_done, m - 1)
                            else:
                                pe.wait_ge(st_done, m + 1)
                        else:
                            pe.wait_ge(ql_done, 4 * m + 4 + 2 * u)
                        queries(m + 1, 1 - bh, 2 * u)
                    values(m, k, bh, u, kind)
                    if ahead and u < 2:
                        pe.wait_ge(ql_done, 4 * m + 4 + 2 * u + 1)
                        queries(m + 1, 1 - bh, 2 * u + 1)
                    if ahead and u == 2:
                        pe.wait_ge(ql_done, 4 * m + 8)
                    if kind != "last":
                        state(m, bh, u, prev)
                    if ahead and u == 2:
                        transposes(1 - bh)
                    if prev and u == GB - 1:
                        if ahead:
                            pe.wait_ge(st_done, m + 2)
                        else:
                            pe.wait_ge(xtl_done, m - 1)
                        x_transposes(m - 1)
                    outputs(m, k, bh, u, prev)

            pe.wait_ge(qs_ready, 1)
            pe.wait_ge(qs_top_done, 1)
            pe.wait_ge(e_t_ready, 1)
            pe.wait_ge(par_ready, 1)
            pe.wait_ge(sl_done, 1)
            for hp in range(HP):
                if hp:
                    pe.wait_ge(ql_done, hp)
                queries(0, 0, hp)
            pe.wait_ge(ql_done, HP)
            transposes(0)
            scores(0, 0, 0, False)
            for bh in range(2):
                step(0, bh, "first")
            with pe.Fori(1, NC - 1) as c:
                for bh in range(2):
                    step(c, bh, "mid")
            for bh in range(2):
                step(NC - 1, bh, "last")
            pe.wait_ge(xtl_done, NG - 1)
            x_transposes(NG - 1)

            pe.wait_ge(feat_sum, 1)
            for c in range(NC):
                nc.tensor.transpose(bank[c // 4][0:D, CH * (c % 4):CH * (c % 4) + CH], feat[:, c, :], ident[:, :]).then_inc(ft_mm, 1)
            pe.wait_ge(small_loaded, 80)
            pe.wait_ge(ft_done, 2)
            pe.wait_ge(fills, 3)
            for c in range(NC):
                o = bank[2][:, EXP * c:EXP * c + EXP]
                mm(o, feat_t[:, CH * c:CH * c + CH], wr_sb[:, :], stop=False)
                mm(o, ones_row[:, :], br_sb[:, :], start=False).then_inc(lg_mm, 1)
            pe.wait_ge(soft, 6)
            for c in range(NC):
                nc.tensor.transpose(bank[3 + c // 4][0:EXP, CH * (c % 4):CH * (c % 4) + CH], gate[:, c, :],
                                    ident[:, :]).then_inc(gt_mm, 1)
            pe.wait_ge(gt_done, 2)
            for i in range(2 * EP):
                if i >= 2:
                    pe.wait_ge(wb_done, i - 1)
                ep, half = i % EP, i // EP
                mm(bank[i % 2][:, :], sel_sb[:, 128 * ep:128 * ep + 128], gate_t[:, GT * half:GT * half + GT]).then_inc(wb_mm, 1)
            for c in range(NC):
                mm(bank[5][:, D * c:D * c + D], gate_t[:, CH * c:CH * c + CH], bo_sb[:, :]).then_inc(wbo_mm, 1)

            def layer1(m, c, bh, ep, free):
                if free or ep >= 2:
                    pe.wait_ge(h1_done, 4 * m + ep - 1)
                o = bank[z1_bank[ep % 2]][:, :]
                cols = slice(128 * ep, 128 * ep + 128)
                mm(o, w1_stack[:, cols], group(x1t_hi, bh, c), stop=False)
                mm(o, w1_stack[:, cols], group(x1t_lo, bh, c), start=False).then_inc(z1_mm, 1)

            def layer2(m, bh, ep, free):
                pe.wait_ge(h1_done, 4 * m + ep + 1)
                if free or ep >= 2:
                    pe.wait_ge(h2r_done, 4 * m + ep - 1)
                mm(bank[z2_bank[ep % 2]][:, :], w2_diag[:, ep, :], h1[:, bh, ep, :]).then_inc(z2_mm, 1)

            def layer3(m, bh, u, free):
                if u == 0:
                    pe.wait_ge(h2w_done, 4 * m + 4)
                    if free:
                        pe.wait_ge(o_y, m - 1)
                for ep in range(EP):
                    last = mm(bank[y_bank[bh]][:, D * u:D * u + D], h2w[:, bh, ep, CH * u:CH * u + CH],
                              wo_pair[:, ep, :], start=(ep == 0), stop=(ep == EP - 1))
                last.then_inc(f3_mm, 1)

            def expert_step(c, bh, kind):
                m = 2 * c + bh
                for ep in range(EP):
                    if not (kind == "last" and bh == 1):
                        layer1(m + 1, c + 1 if bh else c, 1 - bh, ep, True)
                    layer2(m, bh, ep, not (kind == "first" and bh == 0))
                    if not (kind == "first" and bh == 0):
                        layer3(m - 1, 1 - bh, ep, not (kind == "first" or (kind == "second" and bh == 0)))

            pe.wait_ge(ws_ready, 1)
            pe.wait_ge(ws_hi_done, 2)
            pe.wait_ge(xtl_done, NG)
            pe.wait_ge(xth_done, NG)
            pe.wait_ge(wb_done, 2 * EP)
            pe.wait_ge(wbo_done, 1)
            pe.wait_ge(w2_loaded, 32)
            for ep in range(EP):
                layer1(0, 0, 0, ep, False)
            for bh in range(2):
                expert_step(0, bh, "first")
            for bh in range(2):
                expert_step(1, bh, "second")
            with pe.Fori(2, NC - 1) as c:
                for bh in range(2):
                    expert_step(c, bh, "mid")
            for bh in range(2):
                expert_step(NC - 1, bh, "last")
            for u in range(GB):
                layer3(NG - 1, 1, u, True)


_INS = ["x", "L0_tok_W", "L0_attn_Q", "L0_attn_E", "L0_ffn_Wr", "L0_ffn_br", "L0_ffn_W1", "L0_ffn_b1", "L0_ffn_g1",
        "L0_ffn_be1", "L0_ffn_m1", "L0_ffn_v1", "L0_ffn_W2", "L0_ffn_b2", "L0_ffn_g2", "L0_ffn_be2", "L0_ffn_m2",
        "L0_ffn_v2", "L0_ffn_Wo", "L0_ffn_bo"]


def _constants():
    import numpy as np
    t = np.array([[8 * q + 4 * half + s for q in range(2) for s in range(QS)] for half in range(2)])
    angle = 2 * np.pi * np.arange(FREQ)[:, None, None] * t[None] / PATCH
    dft = np.concatenate([np.cos(angle), -np.sin(angle)]) / np.sqrt(PATCH)
    ident = np.eye(128)
    mask = np.triu(np.ones((128, CH)))
    sel = np.repeat(np.eye(EXP), D, axis=1)
    return {n: a.astype(np.float32) for n, a in (("dft", dft), ("ident", ident), ("mask", mask), ("sel", sel))}


def kernel(**inputs):
    import numpy as np
    import concourse.bacc as bacc
    from concourse.bass_utils import run_bass_kernel_spmd

    nc = bacc.Bacc("TRN2", target_bir_lowering=False, num_devices=1)
    arrays, args = {}, []
    given = [(n, np.ascontiguousarray(inputs[n])) for n in _INS] + list(_constants().items())
    for name, a in given:
        arrays[f"in_{name}"] = a
        args.append(nc.dram_tensor(f"in_{name}", a.shape, mybir.dt.from_np(a.dtype), kind="ExternalInput").ap())
    result = nc.dram_tensor("result", (B, NTOK, D), mybir.dt.float32, kind="ExternalOutput").ap()
    build(nc, *args, result)
    r = run_bass_kernel_spmd(nc, [arrays], core_ids=[0])
    return r.results[0]["result"]
```

```python
from contextlib import ExitStack

import concourse.bass as bass
from concourse import mybir

B, C, T, V = 8, 64, 128, 64
PATCH, STRIDE = 16, 8
NPATCH = T // STRIDE
FREQ = PATCH // 2 + 1
GF = 2 * FREQ
D = 64
NTOK = V * NPATCH
CH = 128
NC = NTOK // CH
HEADS = 8
HP = HEADS // 2
EXP = 8
EP = EXP // 2
GB = 4
NG = NC * B // GB
GT = GB * CH
QS = 4
NPAR = 10
LN_EPS = 1e-5
BN_EPS = 1e-3


def build(nc, x, tok_w, att_q, att_e, wr, br, w1, b1, g1, be1, m1, v1, w2, b2, g2, be2, m2, v2, wo, bo,
          dft, ident_in, mask_in, sel_in, fold_in, out):
    f32, f32r = mybir.dt.float32, mybir.dt.float32r
    ALU, ACT, AX = mybir.AluOpType, mybir.ActivationFunctionType, mybir.AxisListType

    ctx = ExitStack()
    with ctx:
        def sb(name, shape, dt=f32, into=ctx):
            return into.enter_context(nc.sbuf_tensor(name, shape, dt))

        def sem(name):
            return ctx.enter_context(nc.semaphore(name))

        ident = sb("ident", [128, 128])
        fold = sb("fold", [128, D])
        mask = sb("mask", [128, CH])
        x1 = sb("x1", [128, NC, B, D])
        feat = sb("feat", [128, NC, D])
        feat_half = sb("feat_half", [128, D])
        w1_stack = sb("w1_stack", [128, EXP * D], f32r)
        w2_hi = sb("w2_hi", [128, EP, 128], f32r)
        w2_lo = sb("w2_lo", [128, EP, 128], f32r)
        wo_pair = sb("wo_pair", [128, EP, D])
        wr_sb = sb("wr_sb", [D, EXP])
        br_sb = sb("br_sb", [128, EXP])
        bo_sb = sb("bo_sb", [EXP, D])
        par_rows = sb("par_rows", [NPAR * EP, 128])
        par = sb("par", [128, NPAR, EP])
        bn_scale = sb("bn_scale", [128, 2, EP])
        bn_bias = sb("bn_bias", [128, 2, EP])
        bn_tmp = sb("bn_tmp", [128, 2, EP])
        eps_ln = sb("eps_ln", [128, 1])
        eps_bn = sb("eps_bn", [128, 1])
        y_ln = sb("y_ln", [128, GB, D])
        xm_ln = sb("xm_ln", [128, GB, D])
        sum_ln = sb("sum_ln", [128, GB])
        mean_ln = sb("mean_ln", [128, GB])
        var_ln = sb("var_ln", [128, GB])
        std_ln = sb("std_ln", [128, GB])
        rstd_ln = sb("rstd_ln", [128, GB])
        xs = sb("xs", [128, GB, 2, D])

        with ExitStack() as early:
            xring = sb("xring", [128, 4, NPATCH, QS * V], into=early)
        x1t_hi = sb("x1t_hi", [128, NC, B, CH], f32r)
        x1t_lo = sb("x1t_lo", [128, NC, B, CH], f32r)

        with ExitStack() as att:
            h_t = sb("h_t", [128, B // 2, NTOK], into=att)
            q_stack = sb("q_stack", [128, HEADS * D], f32r, into=att)
            e_t = sb("e_t", [128, HP, D], into=att)
            s_f = sb("s_f", [128, GB, CH], into=att)
            s_hi = sb("s_hi", [128, 2, GB, CH], f32r, into=att)
            s_lo = sb("s_lo", [128, 2, GB, CH], f32r, into=att)
            s_tok = sb("s_tok", [128, 2, GB, 2, D], into=att)
            with ExitStack() as prep:
                wg = sb("wg", [GF, D, C], into=prep)
                nat = sb("nat", [128, HEADS * D], into=prep)
                nat2 = sb("nat2", [128, HEADS * D], into=prep)
                split_hi = sb("split_hi", [128, HEADS * D], f32r, into=prep)
                w2_diag = sb("w2_diag", [128, EP, 128], into=prep)
                a_w = sb("a_w", [128, 2, QS, D], into=prep)
                a_pad = sb("a_pad", [128, D], into=prep)
                x_edge = sb("x_edge", [128, B, V], into=prep)
                dft_sb = sb("dft_sb", [GF, 2, 2 * QS], into=prep)
                e_nat = sb("e_nat", [D, HP, 2 * D], into=prep)
            q_hi = sb("q_hi", [128, 2, HP, GB, CH], f32r, into=att)
            q_lo = sb("q_lo", [128, 2, HP, GB, CH], f32r, into=att)
            o_sb = sb("o_sb", [128, 2, 2, HP, CH], into=att)
            w_t = sb("w_t", [128, HP, GB, CH], into=att)
            r_t = sb("r_t", [128, GB, CH], into=att)
            g_sum = sb("g_sum", [128, B, D], into=att)
            g_hi = sb("g_hi", [128, B, 128], f32r, into=att)
            g_lo = sb("g_lo", [128, B, 128], f32r, into=att)

        with ExitStack() as ffn:
            sel_sb = sb("sel_sb", [EXP, EP * 128], into=ffn)
            w_bc = sb("w_bc", [128, EP, NTOK], into=ffn)
            feat_t = sb("feat_t", [D, NTOK], into=ffn)
            logit = sb("logit", [128, NC, EXP], into=ffn)
            gate = sb("gate", [128, NC, EXP], into=ffn)
            red = sb("red", [128, 3, NC], into=ffn)
            gate_t = sb("gate_t", [EXP, NTOK], into=ffn)
            wbo = sb("wbo", [128, NC, D], into=ffn)
            h2r = sb("h2r", [128, 2, GT], into=ffn)
            h1 = sb("h1", [128, 2, GT], into=ffn)
            h1_hi = sb("h1_hi", [128, 2, EP, GT], f32r, into=ffn)
            h1_lo = sb("h1_lo", [128, 2, EP, GT], f32r, into=ffn)
            y_t = sb("y_t", [128, GT], into=ffn)
            h2w = sb("h2w", [128, 2, EP, GT], into=ffn)
            o_ln = sb("o_ln", [128, 2, GB, D], into=ffn)

        bank = [ctx.enter_context(nc.psum_tensor(f"bank{i}", [128, 512], f32)) for i in range(8)]

        x_loaded = [[sem(f"x_loaded{i}_{part}") for part in range(2)] for i in range(4)]
        edge_loaded, wg_loaded, dft_loaded = sem("edge_loaded"), sem("wg_loaded"), sem("dft_loaded")
        const_loaded, q_loaded, e_loaded, w1_loaded = (sem("const_loaded"), sem("q_loaded"), sem("e_loaded"),
                                                       sem("w1_loaded"))
        par_loaded, w2_loaded, small_loaded = sem("par_loaded"), sem("w2_loaded"), sem("small_loaded")
        stored = [sem(f"stored{i}") for i in range(2)]
        w2_zeroed, fills, g_zeroed = sem("w2_zeroed"), sem("fills"), sem("g_zeroed")
        a_mm, a_ready, e_t_mm, e_t_ready, par_mm, par_ready = (sem("a_mm"), sem("a_ready"), sem("e_t_mm"),
                                                             sem("e_t_ready"), sem("par_mm"), sem("par_ready"))
        qs_hi_done, qs_top_done, qs_ready = sem("qs_hi_done"), sem("qs_top_done"), sem("qs_ready")
        ws_hi_done, ws_ready, bn_step, bn_sqrt, bn_ready = (sem("ws_hi_done"), sem("ws_ready"), sem("bn_step"),
                                                            sem("bn_sqrt"), sem("bn_ready"))
        tok_mm, ht_act, ht_dve = sem("tok_mm"), sem("ht_act"), sem("ht_dve")
        w2_split = sem("w2_split")
        r_mm, r_done, fold_mm, y_mm, yt_done, yfold_mm = [
            sem(n) for n in ("r_mm", "r_done", "fold_mm", "y_mm", "yt_done", "yfold_mm")]
        rs_done = sem("rs_done")
        h1h_done, h1l_done = sem("h1h_done"), sem("h1l_done")
        sf_done, sh_done, sl_done = sem("sf_done"), sem("sh_done"), sem("sl_done")
        q_mm, qh_done, ql_done = sem("q_mm"), sem("qh_done"), sem("ql_done")
        st_mm, st_done = sem("st_mm"), sem("st_done")
        score_mm, o_done, w_mm, wt_done = sem("score_mm"), sem("o_done"), sem("w_mm"), sem("wt_done")
        g_mm, gsum_done, gh_done, gl_done = sem("g_mm"), sem("gsum_done"), sem("gh_done"), sem("gl_done")
        ln_y, ln_sum, ln_mean, ln_xm, ln_sq, ln_var, ln_std, ln_rstd = [
            sem(n) for n in ("ln_y", "ln_sum", "ln_mean", "ln_xm", "ln_sq", "ln_var", "ln_std", "ln_rstd")]
        xs_done, x1_done, feat_done = sem("xs_done"), sem("x1_done"), sem("feat_done")
        xt_mm, xth_done, xtl_done = sem("xt_mm"), sem("xth_done"), sem("xtl_done")
        sqrt_table, sel_loaded = sem("sqrt_table"), sem("sel_loaded")
        feat_part, ft_mm, ft_done, lg_mm, soft, gate_exp = (sem("feat_part"), sem("ft_mm"), sem("ft_done"),
                                                           sem("lg_mm"), sem("soft"), sem("gate_exp"))
        gt_mm, gt_done, wb_mm, wb_done, wbo_mm, wbo_done, x1b_done = (
            sem("gt_mm"), sem("gt_done"), sem("wb_mm"), sem("wb_done"), sem("wbo_mm"), sem("wbo_done"),
            sem("x1b_done"))
        z1_mm, h1_done, z2_mm, h2r_done, h2w_done = (sem("z1_mm"), sem("h1_done"), sem("z2_mm"), sem("h2r_done"),
                                                     sem("h2w_done"))
        o_y, o_sum, o_mean, o_xm, o_sq, o_var, o_std, o_rstd, o_ready = [
            sem(n) for n in ("o_y", "o_sum", "o_mean", "o_xm", "o_sq", "o_var", "o_std", "o_rstd", "o_ready")]

        def group(ap, bh, c):
            return ap[:, bass.ds(c, 1), GB * bh:GB * bh + GB, :].rearrange("p a b n -> p (a b) n")

        def over_batch(ap, n):
            return ap.unsqueeze(1).broadcast_to((128, GB, n))

        def per_token(ap):
            return ap.unsqueeze(2).broadcast_to((128, GB, D))

        def bank3(i, a):
            return bank[i][:, :].rearrange("p (a b) -> p a b", a=a)

        slots = [xring[:, s, :, :].rearrange("p m (s v) -> p m s v", s=QS) for s in range(4)]
        score_bank, w_bank, r_bank = (0, 1, 2, 3), 5, 6
        z1_bank, z2_bank, yt_bank, y_bank = (0, 1), (2, 3), 4, 5
        feat_bank, logit_bank, gate_bank = (2, 3), 5, (6, 7)
        TOK_TURN, Q_TURN, G_TURN, X_TURN, TURNS = 0, 1, 5, 6, 7

        def turn_bank(bh, turn):
            return (4, 7)[(bh * TURNS + turn) % 2]

        block = ctx.enter_context(nc.Block())

        @block.sync
        def _(sp):
            with nc.allow_non_contiguous_dma(reason="64-channel rows of the tokenizer weight"):
                sp.dma_start(wg[:, :, :], tok_w.rearrange("o (g c) -> g o c", c=C)).then_inc(wg_loaded, 16)
            sp.dma_start(dft_sb[:, :, :], dft).then_inc(dft_loaded, 16)

            parts = (slice(0, NPATCH // 2 + 1), slice(NPATCH // 2 + 1, NPATCH))
            for p in range(B // 2):
                if p >= 2:
                    sp.wait_ge(tok_mm, 4 * (p - 1))
                for part, blocks in enumerate(parts):
                    for b in (2 * p, 2 * p + 1):
                        src = x[b].rearrange("c (m h s) v -> h c m (s v)", h=2, s=QS)
                        for half in range(2):
                            sp.dma_start(xring[64 * half:64 * half + 64, b % 4, blocks, :],
                                         src[half][:, blocks, :]).then_inc(x_loaded[b % 4][part], 16)
                    if p == 0 and part == 0:
                        for half in range(2):
                            sp.dma_start(x_edge[64 * half:64 * half + 64, :, :],
                                         x[:, :, T - 1, :].rearrange("b c v -> c b v")).then_inc(edge_loaded, 16)

            sp.wait_ge(rs_done, NG)
            sp.dma_start(sel_sb[:, :], sel_in).then_inc(sel_loaded, 16)

            out_v = out.rearrange("b (c p) d -> p c b d", p=CH)

            def store(m, c, bh):
                sp.wait_ge(o_ready, m + 1)
                sp.dma_start(group(out_v, bh, c), o_ln[:, bh, :, :]).then_inc(stored[bh], 16)

            with sp.Fori(0, NC) as c:
                for bh in range(2):
                    store(2 * c + bh, c, bh)
            for bh in range(2):
                sp.wait_ge(stored[bh], 16 * NC)

        @block.gpsimd
        def _(pool):
            nc.gpsimd.memset(w2_diag[:, :, :], 0.0).then_inc(w2_zeroed, 1)
            nc.gpsimd.memset(eps_ln[:, :], LN_EPS).then_inc(fills, 1)
            nc.gpsimd.memset(eps_bn[:, :], BN_EPS).then_inc(fills, 1)
            nc.gpsimd.memset(g_sum[:, :, :], 0.0).then_inc(g_zeroed, 1)
            for g in (g_hi, g_lo):
                nc.gpsimd.memset(g[:, :, :].bitcast(f32), 0.0).then_inc(g_zeroed, 1)
            pool.wait_ge(g_zeroed, 3)
            nc.gpsimd.memset(par[:, 0, :], 0.0).then_inc(xtl_done, 1)

            def s_low(m, bh, own):
                pool.wait_ge(sh_done, m + 1)
                if own:
                    pool.wait_ge(*own)
                nc.gpsimd.tensor_tensor(s_lo[:, bh, :, :], s_f[:, :, :], s_hi[:, bh, :, :],
                                        ALU.subtract).then_inc(sl_done, 1)

            def g_low(m, bh, own):
                bs = slice(GB * bh, GB * bh + GB)
                pool.wait_ge(gh_done, 2 * m + 2)
                pool.wait_ge(*own)
                for half in range(2):
                    blk = slice(64 * half, 64 * half + 64)
                    if half:
                        pool.wait_ge(gl_done, 2 * m + 1)
                    nc.gpsimd.tensor_tensor(g_lo[blk, bs, blk], g_sum[blk, bs, :], g_hi[blk, bs, blk],
                                            ALU.subtract).then_inc(gl_done, 1)

            def x1_rows(m, free):
                pool.wait_ge(ln_rstd, m + 1)
                if free:
                    pool.wait_ge(x1_done, m)
                    pool.wait_ge(xt_mm, m)
                    pool.wait_ge(feat_done, m)
                nc.gpsimd.tensor_tensor(xs[:, :, :, :], xm_ln[:, :, :].unsqueeze(2).broadcast_to((128, GB, 2, D)),
                                        rstd_ln[:, :].unsqueeze(2).unsqueeze(3).broadcast_to((128, GB, 2, D)),
                                        ALU.mult).then_inc(xs_done, 1)

            def step(c, bh, kind):
                m = 2 * c + bh
                split = not (kind == "first" and bh == 0) and not (kind == "last" and bh == 1)
                if kind == "last" and bh == 1:
                    pool.wait_ge(gl_done, 2 * (NG - 2))
                if kind != "first":
                    x1_rows(m - 2, kind != "second" or bh == 1)
                if split:
                    g_low(m - 1, 1 - bh, (xs_done, m - 1) if kind != "first" else (sl_done, 3))
                if kind != "last":
                    s_low(m + 2, bh, (gl_done, 2 * m) if split else None)

            s_low(0, 0, None)
            s_low(1, 1, None)
            for bh in range(2):
                step(0, bh, "first")
            for bh in range(2):
                step(1, bh, "second")
            with pool.Fori(2, NC - 1) as c:
                for bh in range(2):
                    step(c, bh, "mid")
            for bh in range(2):
                step(NC - 1, bh, "last")
            def hidden1_low(m, bh, ep):
                pool.wait_ge(h1h_done, 4 * m + ep + 1)
                nc.gpsimd.tensor_tensor(h1_lo[:, bh, ep, :], h1[:, ep % 2, :], h1_hi[:, bh, ep, :],
                                        ALU.subtract).then_inc(h1l_done, 1)

            def add_bias(c, bh):
                rows = group(x1, bh, c)
                nc.gpsimd.tensor_tensor(rows, rows, wbo[:, bass.ds(c, 1), :].broadcast_to((128, GB, D)),
                                        ALU.add).then_inc(x1b_done, 1)

            x1_rows(NG - 2, True)
            hidden1_low(0, 0, 0)
            x1_rows(NG - 1, True)
            for ep in range(1, EP):
                hidden1_low(0, 0, ep)
            pool.wait_ge(x1_done, NG)
            pool.wait_ge(wbo_done, 1)
            add_bias(0, 0)
            for ep in range(EP):
                hidden1_low(1, 1, ep)
            add_bias(0, 1)
            with pool.Fori(1, NC) as c:
                for bh in range(2):
                    for ep in range(EP):
                        hidden1_low(2 * c + bh, bh, ep)
                    add_bias(c, bh)

        @block.scalar
        def _(act):
            act.dma_start(ident[:, :], ident_in).then_inc(const_loaded, 16)
            act.dma_start(mask[:, :], mask_in).then_inc(const_loaded, 16)
            act.dma_start(fold[:, :], fold_in).then_inc(const_loaded, 16)
            for h2 in range(2):
                src = att_e[HP * h2:HP * h2 + HP].rearrange("hp i j -> i hp j")
                act.dma_start(e_nat[:, :, D * h2:D * h2 + D], src).then_inc(e_loaded, 16)
            nat_v = nat[:, :].rearrange("p (hp h2 j) -> p hp h2 j", hp=HP, h2=2)
            for half in range(2):
                rows = slice(64 * half, 64 * half + 64)
                for h2 in range(2):
                    act.dma_start(nat_v[rows, :, h2, :],
                                  att_q[HP * h2:HP * h2 + HP].rearrange("hp i j -> i hp j")).then_inc(q_loaded, 16)
                act.dma_start(nat2[rows, :].rearrange("p (e h) -> p e h", e=EXP),
                              w1.rearrange("e d h -> d e h")).then_inc(w1_loaded, 16)
            for n, p in enumerate((b1, g1, be1, m1, v1, b2, g2, be2, m2, v2)):
                act.dma_start(par_rows[EP * n:EP * n + EP, :],
                              p.rearrange("(ep e2) h -> ep (e2 h)", e2=2)).then_inc(par_loaded, 16)
            act.wait_ge(w2_zeroed, 1)
            w2_v = w2.rearrange("(ep e2) h k -> e2 h ep k", e2=2)
            for e2 in range(2):
                blk = slice(64 * e2, 64 * e2 + 64)
                act.dma_start(w2_diag[blk, :, blk], w2_v[e2]).then_inc(w2_loaded, 16)
            act.dma_start(wo_pair[:, :, :], wo.rearrange("(ep e2) h d -> (e2 h) ep d", e2=2)).then_inc(small_loaded, 16)
            act.dma_start(wr_sb[:, :], wr).then_inc(small_loaded, 16)
            act.dma_start(br_sb[:, :], br.partition_broadcast(128)).then_inc(small_loaded, 16)
            act.dma_start(bo_sb[:, :], bo).then_inc(small_loaded, 16)

            act.wait_ge(q_loaded, 64)
            nc.scalar.activation(split_hi[:, :], nat[:, :], ACT.Copy).then_inc(qs_hi_done, 1)
            nc.scalar.activation(q_stack[0:64, :], nat[0:64, :], ACT.Copy).then_inc(qs_top_done, 1)
            act.wait_ge(w1_loaded, 32)
            act.wait_ge(qs_ready, 1)
            nc.scalar.activation(split_hi[:, :], nat2[:, :], ACT.Copy).then_inc(ws_hi_done, 1)
            nc.scalar.activation(w1_stack[0:64, :], nat2[0:64, :], ACT.Copy).then_inc(ws_hi_done, 1)
            act.wait_ge(w2_loaded, 32)
            nc.scalar.activation(w2_hi[:, :, :], w2_diag[:, :, :], ACT.Copy).then_inc(w2_split, 1)
            def s_high(m, bh, free):
                act.wait_ge(sf_done, m + 1)
                if free:
                    act.wait_ge(score_mm, 8 * m - 8)
                nc.scalar.activation(s_hi[:, bh, :, :], s_f[:, :, :], ACT.Copy).then_inc(sh_done, 1)

            def q_high(m, bh, hp, free):
                act.wait_ge(q_mm, 4 * m + hp + 1)
                if free and hp == 0:
                    act.wait_ge(w_mm, 4 * m - 4)
                nc.scalar.activation(q_hi[:, bh, hp, :, :], bank3(turn_bank(1 - bh, Q_TURN + hp), GB),
                                     ACT.Copy).then_inc(qh_done, 1)

            def s_tokens(m, bh, free):
                act.wait_ge(st_mm, m + 1)
                if free:
                    act.wait_ge(w_mm, 4 * m - 4)
                    act.wait_ge(g_mm, m - 1)
                tok = bank[turn_bank(1 - bh, TOK_TURN)][:, 0:GB * D].rearrange("p (a b) -> p a b", a=GB)
                nc.scalar.activation(s_tok[:, bh, :, :, :], tok.unsqueeze(2).broadcast_to((128, GB, 2, D)),
                                     ACT.Copy).then_inc(st_done, 1)

            def w_copy(m, k, bh, u, free):
                act.wait_ge(w_mm, k + 1)
                if free and u == 0:
                    act.wait_ge(r_mm, m)
                nc.scalar.activation(w_t[:, :, u, :], bank3(w_bank, HP), ACT.Copy).then_inc(wt_done, 1)

            def r_copy(m):
                act.wait_ge(r_mm, m + 1)
                nc.scalar.activation(r_t[:, :, :], bank3(r_bank, GB), ACT.Copy).then_inc(r_done, 1)

            def keep_x1(m, c, bh):
                act.wait_ge(xs_done, m + 1)
                nc.scalar.activation(group(x1, bh, c), xs[:, :, 0, :], ACT.Copy).then_inc(x1_done, 1)

            def g_high(m, bh):
                act.wait_ge(gsum_done, m + 1)
                act.wait_ge(w_mm, 4 * m + 4)
                bs = slice(GB * bh, GB * bh + GB)
                for half in range(2):
                    blk = slice(64 * half, 64 * half + 64)
                    nc.scalar.activation(g_hi[blk, bs, blk], g_sum[blk, bs, :], ACT.Copy).then_inc(gh_done, 1)

            def x_high(m, c, bh, at):
                act.wait_ge(xt_mm, m + 1)
                nc.scalar.activation(group(x1t_hi, bh, c), bank3(at, GB), ACT.Copy).then_inc(xth_done, 1)

            def ln_square(m, s_xm, s_sq):
                act.wait_ge(s_xm, m + 1)
                nc.scalar.activation(y_ln[:, :, :], xm_ln[:, :, :], ACT.Square).then_inc(s_sq, 1)

            def ln_sqrt(m, s_var, s_std):
                act.wait_ge(s_var, m + 1)
                nc.scalar.activation(std_ln[:, :], var_ln[:, :], ACT.Sqrt, bias=eps_ln[:, :],
                                     scale=1.0 / D).then_inc(s_std, 1)

            def step(c, bh, kind):
                m = 2 * c + bh
                prev = not (kind == "first" and bh == 0)
                ahead = not (kind == "last" and bh == 1)
                late = kind != "first"
                for u in range(GB):
                    k = 4 * m + u
                    if late and u == 0:
                        ln_sqrt(m - 2, ln_var, ln_std)
                    if prev and u == 0:
                        r_copy(m - 1)
                    if ahead and u == 0:
                        s_tokens(m + 1, 1 - bh, prev)
                    if ahead and u < 3:
                        q_high(m + 1, 1 - bh, (0, 1, 3)[u], prev)
                    if prev and u == 3:
                        ln_square(m - 1, ln_xm, ln_sq)
                    w_copy(m, k, bh, u, prev)
                    if ahead and u == 1:
                        q_high(m + 1, 1 - bh, 2, prev)
                    if prev and u == 1 and ahead:
                        g_high(m - 1, 1 - bh)
                    if kind != "last" and u == 2:
                        s_high(m + 2, bh, True)
                    if late and u == 2:
                        keep_x1(m - 2, c - 1, bh)
                    if late and u == 3:
                        x_high(m - 2, c - 1, bh, turn_bank(bh, X_TURN))

            hv = h_t[:, :, :].rearrange("p b (v n) -> p b n v", n=NPATCH)

            def tokens(p, g):
                act.wait_ge(tok_mm, 4 * p + 2 * g + 2)
                nc.scalar.activation(hv[0:64, p, 8 * g:8 * g + 8, :], bank3(2 * (p % 2) + g, 8)[0:64],
                                     ACT.Copy).then_inc(ht_act, 1)

            for p in range(2):
                for g in range(2):
                    tokens(p, g)
            act.wait_ge(g_zeroed, 3)
            s_high(0, 0, False)
            act.wait_ge(par_ready, 1)
            act.wait_ge(fills, 2)
            for n in range(2):
                nc.scalar.activation(bn_tmp[:, n, :], par[:, 5 * n + 4, :], ACT.Sqrt, bias=eps_bn[:, :]).then_inc(bn_sqrt, 1)
            tokens(2, 0)
            s_tokens(0, 0, False)
            q_high(0, 0, 0, False)
            q_high(0, 0, 1, False)
            tokens(2, 1)
            q_high(0, 0, 2, False)
            q_high(0, 0, 3, False)
            tokens(3, 0)
            tokens(3, 1)
            s_high(1, 1, False)
            for bh in range(2):
                step(0, bh, "first")
            with act.Fori(1, NC - 1) as c:
                for bh in range(2):
                    step(c, bh, "mid")
            for bh in range(2):
                step(NC - 1, bh, "last")
            def hidden1(m, ep, free):
                act.wait_ge(z1_mm, 4 * m + ep + 1)
                if free or ep >= 2:
                    act.wait_ge(h1l_done, 4 * m + ep - 1)
                nc.scalar.activation(h1[:, ep % 2, :], bank[z1_bank[ep % 2]][:, :], ACT.Relu,
                                     bias=bn_bias[:, 0, ep:ep + 1], scale=bn_scale[:, 0, ep:ep + 1]).then_inc(h1_done, 1)

            def features(i, a, b):
                act.wait_ge(ft_mm, b)
                at = CH * (a - i * NC // 2)
                nc.scalar.activation(feat_t[:, CH * a:CH * b], bank[feat_bank[i]][0:D, at:at + CH * (b - a)], ACT.Copy,
                                     scale=1.0 / B).then_inc(ft_done, 1)

            r_copy(NG - 1)
            ln_sqrt(NG - 2, ln_var, ln_std)
            act.wait_ge(bn_ready, 2)
            for ep in range(2):
                hidden1(0, ep, False)
            keep_x1(NG - 2, NC - 1, 0)
            features(0, 0, NC // 2)
            x_high(NG - 2, NC - 1, 0, turn_bank(0, X_TURN))
            ln_square(NG - 1, ln_xm, ln_sq)
            ln_sqrt(NG - 1, ln_var, ln_std)
            hidden1(0, 2, False)
            features(1, NC // 2, NC - 1)
            keep_x1(NG - 1, NC - 1, 1)
            x_high(NG - 1, NC - 1, 1, turn_bank(1, X_TURN))
            features(1, NC - 1, NC)
            hidden1(0, 3, False)

            act.wait_ge(soft, 3)
            nc.scalar.activation(gate[:, :, :], logit[:, :, :], ACT.Exp).then_inc(gate_exp, 1)
            act.wait_ge(soft, 6)
            nc.scalar.activation(std_ln[:, :], red[:, 2, 0:GB], ACT.Sqrt).then_inc(sqrt_table, 1)
            for i in range(2):
                act.wait_ge(gt_mm, 4 * i + 4)
                nc.scalar.activation(gate_t[:, GT * i:GT * i + GT], bank[feat_bank[i]][0:EXP, :], ACT.Copy).then_inc(gt_done, 1)

            def gate_rows(i):
                act.wait_ge(wb_mm, i + 1)
                nc.scalar.activation(w_bc[:, i % EP, GT * (i // EP):GT * (i // EP) + GT], bank[gate_bank[i % 2]][:, :],
                                     ACT.Copy).then_inc(wb_done, 1)

            for i in range(EP):
                gate_rows(i)

            def hidden2(m, ep, free):
                act.wait_ge(z2_mm, 4 * m + ep + 1)
                if free or ep >= 2:
                    act.wait_ge(h2w_done, 4 * m + ep - 1)
                nc.scalar.activation(h2r[:, ep % 2, :], bank[z2_bank[ep % 2]][:, :], ACT.Relu,
                                     bias=bn_bias[:, 1, ep:ep + 1], scale=bn_scale[:, 1, ep:ep + 1]).then_inc(h2r_done, 1)

            def y_copy(m):
                act.wait_ge(y_mm, m + 1)
                nc.scalar.activation(y_t[:, :], bank[yt_bank][:, :], ACT.Copy).then_inc(yt_done, 1)

            def expert_step(c, bh, kind):
                m = 2 * c + bh
                prev = not (kind == "first" and bh == 0)
                for ep in range(EP):
                    if not (kind == "last" and bh == 1):
                        hidden1(m + 1, ep, True)
                    if prev and ep == 2:
                        y_copy(m - 1)
                    hidden2(m, ep, prev)
                    if not prev:
                        if ep == 0:
                            act.wait_ge(wbo_mm, NC)
                            nc.scalar.activation(wbo[:, :, :], bank3(y_bank, NC), ACT.Copy).then_inc(wbo_done, 1)
                        gate_rows(EP + ep)
                    if kind != "first" and ep == 1:
                        ln_square(m - 2, o_xm, o_sq)
                    if kind != "first" and ep == 3:
                        ln_sqrt(m - 2, o_var, o_std)

            for bh in range(2):
                expert_step(0, bh, "first")
            with act.Fori(1, NC - 1) as c:
                for bh in range(2):
                    expert_step(c, bh, "mid")
            for bh in range(2):
                expert_step(NC - 1, bh, "last")
            ln_square(NG - 2, o_xm, o_sq)
            ln_sqrt(NG - 2, o_var, o_std)
            y_copy(NG - 1)
            ln_square(NG - 1, o_xm, o_sq)
            ln_sqrt(NG - 1, o_var, o_std)

        @block.vector
        def _(dve):
            dve.wait_ge(a_mm, 1)
            for i in range(2):
                src = bank[4 + i][0:64, :].rearrange("p (o h k) -> p h k o", h=2, k=2 * QS)
                for half in range(2):
                    at = a_w[64 * half:64 * half + 64, :, :, D // 2 * i:D // 2 * i + D // 2]
                    nc.vector.tensor_copy(at.rearrange("p q s o -> p (q s) o"), src[:, half]).then_inc(a_ready, 1)
            dve.wait_ge(a_ready, 4)
            nc.vector.tensor_reduce(a_pad[:, :], a_w[:, 1, :, :].rearrange("p s o -> p o s"), AX.X,
                                    ALU.add).then_inc(a_ready, 1)
            dve.wait_ge(q_loaded, 64)
            dve.wait_ge(qs_hi_done, 1)
            nc.vector.tensor_tensor(q_stack[64:128, :], nat[64:128, :], split_hi[64:128, :], ALU.subtract).then_inc(qs_ready, 1)
            dve.wait_ge(w1_loaded, 32)
            dve.wait_ge(ws_hi_done, 1)
            nc.vector.tensor_tensor(w1_stack[64:128, :], nat2[64:128, :], split_hi[64:128, :], ALU.subtract).then_inc(ws_ready, 1)
            dve.wait_ge(w2_split, 1)
            dve.wait_ge(w2_loaded, 32)
            nc.vector.tensor_tensor(w2_lo[:, :, :], w2_diag[:, :, :], w2_hi[:, :, :], ALU.subtract).then_inc(w2_split, 1)
            def s_stage(m, c, bh, free):
                if free:
                    dve.wait_ge(st_mm, m)
                    dve.wait_ge(sl_done, m)
                for j in range(2):
                    src = h_t[64 * j:64 * j + 64, 2 * bh:2 * bh + 2, bass.ds(c * CH, CH)]
                    for half in range(2):
                        dst = s_f[64 * half:64 * half + 64, :, :].rearrange("p (a j) t -> p j a t", j=2)
                        last = nc.vector.tensor_copy(dst[:, j], src)
                last.then_inc(sf_done, 1)

            def q_low(m, bh, hp):
                dve.wait_ge(qh_done, 4 * m + hp + 1)
                nc.vector.tensor_tensor(q_lo[:, bh, hp, :, :], bank3(turn_bank(1 - bh, Q_TURN + hp), GB),
                                        q_hi[:, bh, hp, :, :], ALU.subtract).then_inc(ql_done, 1)

            def mask_scores(k, par_k, free):
                if free:
                    dve.wait_ge(w_mm, k - 1)
                for h2 in range(2):
                    dve.wait_ge(score_mm, 2 * k + h2 + 1)
                    nc.vector.tensor_tensor(o_sb[:, par_k, h2, :, :], bank3(score_bank[2 * par_k + h2], HP),
                                            mask[:, :].unsqueeze(1).broadcast_to((128, HP, CH)),
                                            ALU.mult).then_inc(o_done, 1)

            def ln_first(m, s, y, free):
                nc.vector.tensor_reduce(sum_ln[:, :], y, AX.X, ALU.add).then_inc(s["sum"], 1)
                dve.wait_ge(s["sum"], m + 1)
                nc.vector.tensor_scalar(mean_ln[:, :], sum_ln[:, :], 1.0 / D, None, ALU.mult).then_inc(s["mean"], 1)
                dve.wait_ge(s["mean"], m + 1)
                if free:
                    dve.wait_ge(xs_done, m)
                nc.vector.tensor_tensor(xm_ln[:, :, :], y, per_token(mean_ln[:, :]),
                                        ALU.subtract).then_inc(s["xm"], 1)

            def ln_var_sum(m, s):
                dve.wait_ge(s["sq"], m + 1)
                nc.vector.tensor_reduce(var_ln[:, :], y_ln[:, :, :], AX.X, ALU.add).then_inc(s["var"], 1)

            def ln_reciprocal(m, s):
                dve.wait_ge(s["std"], m + 1)
                nc.vector.reciprocal(rstd_ln[:, :], std_ln[:, :]).then_inc(s["rstd"], 1)

            ln1 = dict(sum=ln_sum, mean=ln_mean, xm=ln_xm, sq=ln_sq, var=ln_var, std=ln_std, rstd=ln_rstd)
            ln2 = dict(sum=o_sum, mean=o_mean, xm=o_xm, sq=o_sq, var=o_var, std=o_std, rstd=o_rstd)

            def add_tokens(m, c, bh):
                dve.wait_ge(r_done, m + 1)
                for j in range(2):
                    at = r_t[64 * j:64 * j + 64, :, :].rearrange("p (a j) t -> p j a t", j=2)[:, j]
                    last = nc.vector.tensor_tensor(at, at, h_t[64 * j:64 * j + 64, 2 * bh:2 * bh + 2,
                                                               bass.ds(c * CH, CH)], ALU.add)
                last.then_inc(rs_done, 1)

            def center(m, free):
                dve.wait_ge(fold_mm, m + 1)
                ln_first(m, ln1, bank[r_bank][:, 0:GB * D].rearrange("p (a b) -> p a b", a=GB), free)

            def g_add(m, bh, free):
                dve.wait_ge(g_mm, m + 1)
                if free:
                    dve.wait_ge(gl_done, 2 * m)
                bs = slice(GB * bh, GB * bh + GB)
                nc.vector.tensor_tensor(g_sum[:, bs, :], g_sum[:, bs, :],
                                        bank[turn_bank(bh, G_TURN)][:, 0:GB * D].rearrange("p (a b) -> p a b", a=GB),
                                        ALU.add).then_inc(gsum_done, 1)

            def feature_sum(m, c, bh):
                dve.wait_ge(xs_done, m + 1)
                rows = xs[:, :, 0, :].rearrange("p b d -> p d b")
                at = feat[:, bass.ds(c, 1), :].rearrange("p a d -> p (a d)")
                if bh == 0:
                    nc.vector.tensor_reduce(at, rows, AX.X, ALU.add).then_inc(feat_done, 1)
                else:
                    nc.vector.tensor_reduce(feat_half[:, :], rows, AX.X, ALU.add).then_inc(feat_part, 1)
                    dve.wait_ge(feat_part, c + 1)
                    nc.vector.tensor_tensor(at, at, feat_half[:, :], ALU.add).then_inc(feat_done, 1)

            def x_low(m, c, bh, at):
                dve.wait_ge(xth_done, m + 1)
                nc.vector.tensor_tensor(group(x1t_lo, bh, c), bank3(at, GB), group(x1t_hi, bh, c),
                                        ALU.subtract).then_inc(xtl_done, 1)

            def step(c, bh, kind):
                m = 2 * c + bh
                prev = not (kind == "first" and bh == 0)
                ahead = not (kind == "last" and bh == 1)
                late = kind != "first"
                for u in range(GB):
                    k = 4 * m + u
                    if ahead or u < GB - 1:
                        mask_scores(k + 1, (u + 1) % 2, prev or u >= 1)
                    if late and u == 0:
                        ln_reciprocal(m - 2, ln1)
                    if prev and u == 0:
                        add_tokens(m - 1, c if bh else c - 1, 1 - bh)
                    if kind != "last" and u == 1:
                        s_stage(m + 2, c + 1, bh, True)
                    if ahead and u < 3:
                        q_low(m + 1, 1 - bh, (0, 1, 3)[u])
                    if ahead and u == 1:
                        q_low(m + 1, 1 - bh, 2)
                    if prev and u == 2:
                        center(m - 1, late)
                    if kind != "last" and u == 3:
                        g_add(m, bh, kind != "first" or bh == 1)
                    if prev and u == 3:
                        ln_var_sum(m - 1, ln1)
                    if late and u == 3:
                        feature_sum(m - 2, c - 1, bh)
                        x_low(m - 2, c - 1, bh, turn_bank(bh, X_TURN))

            hv = h_t[:, :, :].rearrange("p b (v n) -> p b n v", n=NPATCH)

            def tokens(p, g):
                dve.wait_ge(tok_mm, 4 * p + 2 * g + 2)
                nc.vector.tensor_copy(hv[64:128, p, 8 * g:8 * g + 8, :],
                                      bank3(2 * (p % 2) + g, 8)[64:128]).then_inc(ht_dve, 1)

            tokens(0, 0)
            tokens(0, 1)
            dve.wait_ge(e_t_mm, 1)
            nc.vector.tensor_copy(e_t[:, :, :], bank[6][:, 0:HP * D].rearrange("p (a b) -> p a b", a=HP)).then_inc(e_t_ready, 1)
            tokens(1, 0)
            tokens(1, 1)
            dve.wait_ge(ht_dve, B // 2)
            dve.wait_ge(ht_act, B // 2)
            s_stage(0, 0, 0, False)
            dve.wait_ge(par_mm, 1)
            dve.wait_ge(xtl_done, 1)
            nc.vector.tensor_copy(par[:, :, :].rearrange("p n e -> p (n e)"), bank[5][:, 0:NPAR * EP]).then_inc(par_ready, 1)
            dve.wait_ge(bn_sqrt, 2)
            dve.wait_ge(par_ready, 1)
            nc.vector.reciprocal(bn_scale[:, :, :], bn_tmp[:, :, :]).then_inc(bn_step, 1)
            for n in range(2):
                dve.wait_ge(bn_step, 4 * n + 1)
                nc.vector.tensor_tensor(bn_scale[:, n, :], bn_scale[:, n, :], par[:, 5 * n + 1, :], ALU.mult).then_inc(bn_step, 1)
                nc.vector.tensor_tensor(bn_bias[:, n, :], par[:, 5 * n, :], par[:, 5 * n + 3, :], ALU.subtract).then_inc(bn_step, 1)
                dve.wait_ge(bn_step, 4 * n + 3)
                nc.vector.tensor_tensor(bn_bias[:, n, :], bn_bias[:, n, :], bn_scale[:, n, :], ALU.mult).then_inc(bn_step, 1)
                dve.wait_ge(bn_step, 4 * n + 4)
                nc.vector.tensor_tensor(bn_bias[:, n, :], bn_bias[:, n, :], par[:, 5 * n + 2, :], ALU.add).then_inc(bn_step, 1)
            dve.wait_ge(bn_step, 9)
            nc.vector.tensor_copy(bn_tmp[:, 0, :], bn_bias[:, 0, :]).then_inc(bn_ready, 2)

            dve.wait_ge(const_loaded, 48)
            tokens(2, 0)
            q_low(0, 0, 0)
            q_low(0, 0, 1)
            tokens(2, 1)
            q_low(0, 0, 2)
            q_low(0, 0, 3)
            tokens(3, 0)
            mask_scores(0, 0, False)
            tokens(3, 1)
            dve.wait_ge(ht_dve, B)
            dve.wait_ge(ht_act, B)
            s_stage(1, 0, 1, True)
            for bh in range(2):
                step(0, bh, "first")
            with dve.Fori(1, NC - 1) as c:
                for bh in range(2):
                    step(c, bh, "mid")
            for bh in range(2):
                step(NC - 1, bh, "last")
            def hidden1_high(m, bh, ep, free):
                dve.wait_ge(h1_done, 4 * m + ep + 1)
                if free and ep == 0:
                    dve.wait_ge(z2_mm, 4 * m - 4)
                nc.vector.tensor_copy(h1_hi[:, bh, ep, :], h1[:, ep % 2, :]).then_inc(h1h_done, 1)

            add_tokens(NG - 1, NC - 1, 1)
            ln_reciprocal(NG - 2, ln1)
            hidden1_high(0, 0, 0, False)
            hidden1_high(0, 0, 1, False)
            center(NG - 1, True)
            feature_sum(NG - 2, NC - 1, 0)
            ln_var_sum(NG - 1, ln1)
            ln_reciprocal(NG - 1, ln1)
            x_low(NG - 2, NC - 1, 0, turn_bank(0, X_TURN))
            hidden1_high(0, 0, 2, False)
            feature_sum(NG - 1, NC - 1, 1)
            x_low(NG - 1, NC - 1, 1, turn_bank(1, X_TURN))
            hidden1_high(0, 0, 3, False)

            dve.wait_ge(lg_mm, NC)
            dve.wait_ge(small_loaded, 64)
            ps_lg = bank[logit_bank][:, 0:NC * EXP].rearrange("p (c e) -> p c e", e=EXP)
            nc.vector.tensor_tensor(logit[:, :, :], ps_lg, br_sb[:, :].unsqueeze(1).broadcast_to((128, NC, EXP)),
                                    ALU.add).then_inc(soft, 1)
            dve.wait_ge(soft, 1)
            nc.vector.tensor_reduce(red[:, 0, :], logit[:, :, :], AX.X, ALU.max).then_inc(soft, 1)
            dve.wait_ge(soft, 2)
            nc.vector.tensor_tensor(logit[:, :, :], logit[:, :, :],
                                    red[:, 0, :].unsqueeze(2).broadcast_to((128, NC, EXP)), ALU.subtract).then_inc(soft, 1)
            dve.wait_ge(gate_exp, 1)
            nc.vector.tensor_reduce(red[:, 1, :], gate[:, :, :], AX.X, ALU.add).then_inc(soft, 1)
            dve.wait_ge(soft, 4)
            nc.vector.reciprocal(red[:, 2, :], red[:, 1, :]).then_inc(soft, 1)
            dve.wait_ge(soft, 5)
            nc.vector.tensor_tensor(gate[:, :, :], gate[:, :, :],
                                    red[:, 2, :].unsqueeze(2).broadcast_to((128, NC, EXP)), ALU.mult).then_inc(soft, 1)

            def gate_hidden(m, c, bh, ep, free):
                dve.wait_ge(h2r_done, 4 * m + ep + 1)
                if free and ep == 0:
                    dve.wait_ge(y_mm, m - 1)
                nc.vector.tensor_tensor(
                    h2w[:, bh, ep, :].rearrange("p (b t) -> p b t", b=GB),
                    h2r[:, ep % 2, :].rearrange("p (b t) -> p b t", b=GB),
                    w_bc[:, ep, bass.ds(c * CH, CH)].unsqueeze(1).broadcast_to((128, GB, CH)),
                    ALU.mult).then_inc(h2w_done, 1)

            def out_residual(m, c, bh):
                dve.wait_ge(yfold_mm, m + 1)
                dve.wait_ge(x1b_done, m + 1)
                nc.vector.tensor_tensor(y_ln[:, :, :],
                                        bank[y_bank][:, 0:GB * D].rearrange("p (a b) -> p a b", a=GB),
                                        group(x1, bh, c), ALU.add).then_inc(o_y, 1)

            def out_center(m):
                dve.wait_ge(o_y, m + 1)
                ln_first(m, ln2, y_ln[:, :, :], False)

            def out_scale(m, c, bh, free):
                if free:
                    dve.wait_ge(stored[bh], 16 * c)
                ln_reciprocal(m, ln2)
                dve.wait_ge(o_rstd, m + 1)
                nc.vector.tensor_tensor(o_ln[:, bh, :, :], xm_ln[:, :, :], per_token(rstd_ln[:, :]),
                                        ALU.mult).then_inc(o_ready, 1)

            def expert_step(c, bh, kind):
                m = 2 * c + bh
                late = kind != "first"
                for ep in range(EP):
                    if not (kind == "last" and bh == 1):
                        hidden1_high(m + 1, 1 - bh, ep, late or bh == 1)
                    gate_hidden(m, c, bh, ep, late)
                    if late:
                        if ep == 0:
                            out_residual(m - 2, c - 1, bh)
                            out_center(m - 2)
                        if ep == 2:
                            ln_var_sum(m - 2, ln2)
                        if ep == 3:
                            out_scale(m - 2, c - 1, bh, kind != "second")

            dve.wait_ge(wb_done, EP)
            for bh in range(2):
                expert_step(0, bh, "first")
            dve.wait_ge(wb_done, 2 * EP)
            for bh in range(2):
                expert_step(1, bh, "second")
            with dve.Fori(2, NC - 1) as c:
                for bh in range(2):
                    expert_step(c, bh, "mid")
            for bh in range(2):
                expert_step(NC - 1, bh, "last")
            for m in (NG - 2, NG - 1):
                out_residual(m, NC - 1, m % 2)
                out_center(m)
                ln_var_sum(m, ln2)
                out_scale(m, NC - 1, m % 2, True)

        @block.tensor
        def _(pe):
            def mm(o, lhs_t, rhs, start=True, stop=True):
                return nc.tensor.matmul(o, lhs_t, rhs, start=start, stop=stop, skip_group_check=True)

            pe.wait_ge(wg_loaded, 16)
            pe.wait_ge(dft_loaded, 16)
            for o in range(D):
                last = mm(bank[4 + 2 * o // D][0:64, 4 * QS * (o % (D // 2)):4 * QS * (o % (D // 2) + 1)], wg[:, o, :],
                          dft_sb[:, :, :].rearrange("g h k -> g (h k)"))
            last.then_inc(a_mm, 1)

            def tokens(p, g):
                for b in (2 * p, 2 * p + 1):
                    pe.wait_ge(x_loaded[b % 4][g], 32 * (b // 4 + 1))
                if p >= 2:
                    pe.wait_ge(ht_act, 2 * (p - 2) + g + 1)
                    pe.wait_ge(ht_dve, 2 * (p - 2) + g + 1)
                ps = bank3(2 * (p % 2) + g, 8)
                for q in range(2):
                    n = 8 if q == 0 or g == 0 else 7
                    for s in range(QS):
                        for j in range(2):
                            end = g == 0 and q == 1 and s == QS - 1
                            last = mm(ps[64 * j:64 * j + 64, 0:n, :], a_w[:, q, s, :],
                                      slots[(2 * p + j) % 4][:, 8 * g + q:8 * g + q + n, s, :], start=(q + s == 0),
                                      stop=end)
                            if end:
                                last.then_inc(tok_mm, 1)
                if g == 1:
                    if p == 0:
                        pe.wait_ge(edge_loaded, 32)
                    for j in range(2):
                        mm(ps[64 * j:64 * j + 64, 7, :], a_pad[:, :], x_edge[:, 2 * p + j, :],
                           start=False).then_inc(tok_mm, 1)

            def queries(m, bh, hp):
                cols = slice(128 * hp, 128 * hp + 128)
                o = bank[turn_bank(1 - bh, Q_TURN + hp)][:, :]
                mm(o, q_stack[:, cols], s_hi[:, bh, :, :], stop=False)
                mm(o, q_stack[:, cols], s_lo[:, bh, :, :], start=False).then_inc(q_mm, 1)

            def transposes(bh):
                for u in range(GB):
                    last = nc.tensor.transpose(bank[turn_bank(1 - bh, TOK_TURN)][:, D * u:D * u + D], s_f[0:D, u, :],
                                               ident[0:D, 0:D])
                last.then_inc(st_mm, 1)

            def scores(k, bh, u, free):
                for h2 in range(2):
                    rows = slice(64 * h2, 64 * h2 + 64)
                    if free:
                        pe.wait_ge(o_done, 2 * k - 3 + h2)
                    o = bank[score_bank[2 * (u % 2) + h2]][:, :]
                    mm(o, s_hi[rows, bh, u, :], q_hi[rows, bh, :, u, :], stop=False)
                    mm(o, s_hi[rows, bh, u, :], q_lo[rows, bh, :, u, :], start=False, stop=False)
                    mm(o, s_lo[rows, bh, u, :], q_hi[rows, bh, :, u, :], start=False).then_inc(score_mm, 1)

            def values(m, k, bh, u, kind):
                if not (kind == "first" and bh == 0 and u == 0):
                    pe.wait_ge(wt_done, k)
                inter = kind != "first"
                if inter:
                    if u == 0:
                        pe.wait_ge(gl_done, 2 * m - 2)
                    b = GB * bh + u
                    mm(bank[w_bank][:, :], g_hi[:, b, :], q_hi[:, bh, :, u, :], stop=False)
                    mm(bank[w_bank][:, :], g_hi[:, b, :], q_lo[:, bh, :, u, :], start=False, stop=False)
                    mm(bank[w_bank][:, :], g_lo[:, b, :], q_hi[:, bh, :, u, :], start=False, stop=False)
                if u == 0:
                    pe.wait_ge(st_done, m + 1)
                for h2 in range(2):
                    pe.wait_ge(o_done, 2 * k + h2 + 1)
                    last = mm(bank[w_bank][64 * h2:64 * h2 + 64, :], s_tok[:, bh, u, 0, :], o_sb[:, u % 2, h2, :, :],
                              start=not inter)
                last.then_inc(w_mm, 1)

            def state(bh):
                for u in range(GB):
                    last = mm(bank[turn_bank(bh, G_TURN)][:, D * u:D * u + D],
                              s_tok[:, bh, u, :, :].rearrange("p r d -> p (r d)"), s_tok[:, bh, u, 0, :])
                last.then_inc(g_mm, 1)

            def outputs(m, bh, free):
                pe.wait_ge(wt_done, 4 * m + 4)
                if free:
                    pe.wait_ge(ln_xm, m)
                for hp in range(HP):
                    half = hp % 2
                    last = mm(bank[r_bank][64 * half:64 * half + 64, :], e_t[:, hp, :], w_t[:, hp, :, :],
                              start=(hp < 2), stop=(hp >= 2))
                last.then_inc(r_mm, 1)

            def fold_rows(at, rows, done):
                for u in range(GB):
                    last = mm(bank[at][:, D * u:D * u + D], rows(u), fold[:, :])
                last.then_inc(done, 1)

            def fold_r(m):
                pe.wait_ge(rs_done, m + 1)
                fold_rows(r_bank, lambda u: r_t[:, u, :], fold_mm)

            def x_transposes(m, at):
                pe.wait_ge(xs_done, m + 1)
                for u in range(GB):
                    last = nc.tensor.transpose(bank[at][:, CH * u:CH * u + CH],
                                               xs[:, u, :, :].rearrange("p r d -> p (r d)"), ident[:, :])
                last.then_inc(xt_mm, 1)

            def step(c, bh, kind):
                m = 2 * c + bh
                prev = not (kind == "first" and bh == 0)
                ahead = not (kind == "last" and bh == 1)
                late = kind != "first"
                for u in range(GB):
                    k = 4 * m + u
                    if ahead or u < GB - 1:
                        if u == GB - 1:
                            pe.wait_ge(ql_done, 4 * m + 8)
                        scores(k + 1, bh if u < GB - 1 else 1 - bh, (u + 1) % GB, prev or u >= 1)
                    if ahead and u == 0:
                        pe.wait_ge(sf_done, m + 2)
                        if prev:
                            pe.wait_ge(gsum_done, m)
                    if prev and u == 0:
                        outputs(m - 1, 1 - bh, late)
                    if ahead and u == 0:
                        transposes(1 - bh)
                        pe.wait_ge(sl_done, m + 2)
                        if late:
                            pe.wait_ge(xtl_done, m - 1)
                        queries(m + 1, 1 - bh, 0)
                    if ahead and u == 1:
                        pe.wait_ge(st_done, m + 2)
                        queries(m + 1, 1 - bh, 1)
                    if ahead and u == 2:
                        pe.wait_ge(ql_done, 4 * m + 6)
                        queries(m + 1, 1 - bh, 3)
                    values(m, k, bh, u, kind)
                    if ahead and u == 1:
                        pe.wait_ge(ql_done, 4 * m + 5)
                        queries(m + 1, 1 - bh, 2)
                    if prev and u == 1:
                        fold_r(m - 1)
                    if kind != "last" and u == 2:
                        pe.wait_ge(ql_done, 4 * m + 7)
                        state(bh)
                    if late and u == 3:
                        x_transposes(m - 2, turn_bank(bh, X_TURN))

            pe.wait_ge(a_ready, 5)
            tokens(0, 0)
            tokens(0, 1)
            pe.wait_ge(const_loaded, 48)
            pe.wait_ge(e_loaded, 32)
            for hp in range(HP):
                last = nc.tensor.transpose(bank[6][:, D * hp:D * hp + D], e_nat[:, hp, :], ident[0:D, 0:D])
            last.then_inc(e_t_mm, 1)
            tokens(1, 0)
            tokens(1, 1)
            pe.wait_ge(par_loaded, 16 * NPAR)
            nc.tensor.transpose(bank[5][:, 0:NPAR * EP], par_rows[:, :], ident[0:NPAR * EP, 0:NPAR * EP]).then_inc(par_mm, 1)
            tokens(2, 0)
            pe.wait_ge(sf_done, 1)
            transposes(0)
            pe.wait_ge(qs_ready, 1)
            pe.wait_ge(qs_top_done, 1)
            pe.wait_ge(sl_done, 1)
            queries(0, 0, 0)
            pe.wait_ge(st_done, 1)
            queries(0, 0, 1)
            tokens(2, 1)
            for hp in range(2, HP):
                pe.wait_ge(ql_done, hp - 1)
                queries(0, 0, hp)
            tokens(3, 0)
            pe.wait_ge(ql_done, HP)
            pe.wait_ge(ht_act, B - 2)
            pe.wait_ge(ht_dve, B - 2)
            scores(0, 0, 0, False)
            tokens(3, 1)
            pe.wait_ge(ht_act, B)
            pe.wait_ge(ht_dve, B)
            pe.wait_ge(e_t_ready, 1)
            pe.wait_ge(par_ready, 1)
            for bh in range(2):
                step(0, bh, "first")
            with pe.Fori(1, NC - 1) as c:
                for bh in range(2):
                    step(c, bh, "mid")
            for bh in range(2):
                step(NC - 1, bh, "last")
            def layer1(m, c, bh, ep, free):
                if free or ep >= 2:
                    pe.wait_ge(h1_done, 4 * m + ep - 1)
                o = bank[z1_bank[ep % 2]][:, :]
                cols = slice(128 * ep, 128 * ep + 128)
                mm(o, w1_stack[:, cols], group(x1t_hi, bh, c), stop=False)
                mm(o, w1_stack[:, cols], group(x1t_lo, bh, c), start=False).then_inc(z1_mm, 1)

            def features(a, b):
                pe.wait_ge(feat_done, 2 * b)
                for c in range(a, b):
                    at = CH * (c % (NC // 2))
                    nc.tensor.transpose(bank[feat_bank[2 * c // NC]][0:D, at:at + CH], feat[:, c, :],
                                        ident[:, :]).then_inc(ft_mm, 1)

            def logits(a, b, done):
                pe.wait_ge(ft_done, done)
                for c in range(a, b):
                    mm(bank[logit_bank][:, EXP * c:EXP * c + EXP], feat_t[:, CH * c:CH * c + CH],
                       wr_sb[:, :]).then_inc(lg_mm, 1)

            outputs(NG - 1, 1, True)
            pe.wait_ge(ws_ready, 1)
            pe.wait_ge(ws_hi_done, 2)
            for ep in range(2):
                layer1(0, 0, 0, ep, False)
            fold_r(NG - 1)
            features(0, NC // 2)
            pe.wait_ge(xtl_done, NG - 2)
            x_transposes(NG - 2, turn_bank(0, X_TURN))
            pe.wait_ge(small_loaded, 64)
            logits(0, NC // 2, 1)
            for ep in range(2, EP):
                layer1(0, 0, 0, ep, False)
            features(NC // 2, NC - 1)
            logits(NC // 2, NC - 1, 2)
            pe.wait_ge(xtl_done, NG - 1)
            x_transposes(NG - 1, turn_bank(1, X_TURN))
            features(NC - 1, NC)
            logits(NC - 1, NC, 3)

            pe.wait_ge(soft, 6)
            for c in range(NC):
                at = CH * (c % (NC // 2))
                nc.tensor.transpose(bank[feat_bank[2 * c // NC]][0:EXP, at:at + CH], gate[:, c, :],
                                    ident[:, :]).then_inc(gt_mm, 1)
            pe.wait_ge(gt_done, 2)
            pe.wait_ge(sel_loaded, 16)

            def gate_rows(i):
                if i >= 2:
                    pe.wait_ge(wb_done, i - 1)
                ep, half = i % EP, i // EP
                mm(bank[gate_bank[i % 2]][:, :], sel_sb[:, 128 * ep:128 * ep + 128],
                   gate_t[:, GT * half:GT * half + GT]).then_inc(wb_mm, 1)

            for i in range(EP):
                gate_rows(i)

            def layer2(m, bh, ep, free):
                pe.wait_ge(h1l_done, 4 * m + ep + 1)
                if free or ep >= 2:
                    pe.wait_ge(h2r_done, 4 * m + ep - 1)
                o = bank[z2_bank[ep % 2]][:, :]
                mm(o, w2_hi[:, ep, :], h1_hi[:, bh, ep, :], stop=False)
                mm(o, w2_lo[:, ep, :], h1_hi[:, bh, ep, :], start=False, stop=False)
                mm(o, w2_hi[:, ep, :], h1_lo[:, bh, ep, :], start=False).then_inc(z2_mm, 1)

            def layer3(m, bh, free):
                pe.wait_ge(h2w_done, 4 * m + 4)
                if free:
                    pe.wait_ge(yt_done, m)
                for ep in range(EP):
                    half = ep % 2
                    last = mm(bank[yt_bank][64 * half:64 * half + 64, :], wo_pair[:, ep, :], h2w[:, bh, ep, :],
                              start=(ep < 2), stop=(ep >= 2))
                last.then_inc(y_mm, 1)

            def fold_y(m, free):
                pe.wait_ge(yt_done, m + 1)
                if free:
                    pe.wait_ge(o_y, m)
                fold_rows(y_bank, lambda u: y_t[:, CH * u:CH * u + CH], yfold_mm)

            def expert_step(c, bh, kind):
                m = 2 * c + bh
                prev = not (kind == "first" and bh == 0)
                for ep in range(EP):
                    if not (kind == "last" and bh == 1):
                        layer1(m + 1, c + 1 if bh else c, 1 - bh, ep, True)
                    layer2(m, bh, ep, prev)
                    if not prev:
                        if ep == 0:
                            for n in range(NC):
                                mm(bank[y_bank][:, D * n:D * n + D], gate_t[:, CH * n:CH * n + CH],
                                   bo_sb[:, :]).then_inc(wbo_mm, 1)
                        gate_rows(EP + ep)
                    if prev and ep == 1:
                        layer3(m - 1, 1 - bh, kind != "first")
                    if prev and ep == 3:
                        fold_y(m - 1, kind != "first")

            pe.wait_ge(xtl_done, NG + 1)
            pe.wait_ge(xth_done, NG)
            pe.wait_ge(w2_split, 2)
            for bh in range(2):
                expert_step(0, bh, "first")
            with pe.Fori(1, NC - 1) as c:
                for bh in range(2):
                    expert_step(c, bh, "mid")
            for bh in range(2):
                expert_step(NC - 1, bh, "last")
            layer3(NG - 1, 1, True)
            fold_y(NG - 1, True)


_INS = ["x", "L0_tok_W", "L0_attn_Q", "L0_attn_E", "L0_ffn_Wr", "L0_ffn_br", "L0_ffn_W1", "L0_ffn_b1", "L0_ffn_g1",
        "L0_ffn_be1", "L0_ffn_m1", "L0_ffn_v1", "L0_ffn_W2", "L0_ffn_b2", "L0_ffn_g2", "L0_ffn_be2", "L0_ffn_m2",
        "L0_ffn_v2", "L0_ffn_Wo", "L0_ffn_bo"]


def _constants():
    import numpy as np
    t = np.array([[8 * q + 4 * half + s for q in range(2) for s in range(QS)] for half in range(2)])
    angle = 2 * np.pi * np.arange(FREQ)[:, None, None] * t[None] / PATCH
    dft = np.concatenate([np.cos(angle), -np.sin(angle)]) / np.sqrt(PATCH)
    ident = np.eye(128)
    mask = np.triu(np.ones((128, CH)))
    sel = np.repeat(np.eye(EXP), D, axis=1)
    fold = np.concatenate([np.eye(D), np.eye(D)])
    return {n: a.astype(np.float32) for n, a in (("dft", dft), ("ident", ident), ("mask", mask), ("sel", sel), ("fold", fold))}


def kernel(**inputs):
    import numpy as np
    import concourse.bacc as bacc
    from concourse.bass_utils import run_bass_kernel_spmd

    nc = bacc.Bacc("TRN2", target_bir_lowering=False, num_devices=1)
    arrays, args = {}, []
    given = [(n, np.ascontiguousarray(inputs[n])) for n in _INS] + list(_constants().items())
    for name, a in given:
        arrays[f"in_{name}"] = a
        args.append(nc.dram_tensor(f"in_{name}", a.shape, mybir.dt.from_np(a.dtype), kind="ExternalInput").ap())
    result = nc.dram_tensor("result", (B, NTOK, D), mybir.dt.float32, kind="ExternalOutput").ap()
    build(nc, *args, result)
    r = run_bass_kernel_spmd(nc, [arrays], core_ids=[0])
    return r.results[0]["result"]
```

```python
from contextlib import ExitStack

import concourse.bass as bass
from concourse import mybir

B, C, T, V = 8, 64, 128, 64
PATCH, STRIDE = 16, 8
NPATCH = T // STRIDE
FREQ = PATCH // 2 + 1
GF = 2 * FREQ
D = 64
NTOK = V * NPATCH
CH = 128
NC = NTOK // CH
HEADS = 8
HP = HEADS // 2
EXP = 8
EP = EXP // 2
GB = 4
NG = NC * B // GB
GT = GB * CH
QS = 4
NPAR = 10
LN_EPS = 1e-5
BN_EPS = 1e-3
GS = 32 + EXP


def build(nc, x, tok_w, att_q, att_e, wr, br, w1, b1, g1, be1, m1, v1, w2, b2, g2, be2, m2, v2, wo, bo,
          dft, ident_in, mask_in, sel_in, fold_in, out):
    f32, f32r = mybir.dt.float32, mybir.dt.float32r
    ALU, ACT, AX = mybir.AluOpType, mybir.ActivationFunctionType, mybir.AxisListType

    ctx = ExitStack()
    with ctx:
        def sb(name, shape, dt=f32, into=ctx):
            return into.enter_context(nc.sbuf_tensor(name, shape, dt))

        def sem(name):
            return ctx.enter_context(nc.semaphore(name))

        ident = sb("ident", [128, 128])
        fold = sb("fold", [128, D])
        mask = sb("mask", [128, CH])
        x1 = sb("x1", [128, NC, B, D])
        feat = sb("feat", [128, NC, D])
        feat_half = sb("feat_half", [128, D])
        w1_stack = sb("w1_stack", [128, EXP * D], f32r)
        w2_hi = sb("w2_hi", [128, EP, 128], f32r)
        w2_lo = sb("w2_lo", [128, EP, 128], f32r)
        wr_sb = sb("wr_sb", [D, EXP])
        br_sb = sb("br_sb", [128, EXP])
        bo_sb = sb("bo_sb", [EXP, D])
        par_rows = sb("par_rows", [NPAR * EP, 128])
        par = sb("par", [128, NPAR, EP])
        bn_scale = sb("bn_scale", [128, 2, EP])
        bn_bias = sb("bn_bias", [128, 2, EP])
        bn_tmp = sb("bn_tmp", [128, 2, EP])
        eps_ln = sb("eps_ln", [128, 1])
        eps_bn = sb("eps_bn", [128, 1])
        y_ln = sb("y_ln", [128, GB, D])
        xm_ln = sb("xm_ln", [128, GB, D])
        sum_ln = sb("sum_ln", [128, GB])
        mean_ln = sb("mean_ln", [128, GB])
        var_ln = sb("var_ln", [128, GB])
        std_ln = sb("std_ln", [128, GB])
        rstd_ln = sb("rstd_ln", [128, GB])
        xs = sb("xs", [128, GB, 2, D])

        with ExitStack() as early:
            xring = sb("xring", [128, 4, NPATCH, QS * V], into=early)
        x1t_hi = sb("x1t_hi", [128, NC, B, CH], f32r)
        x1t_lo = sb("x1t_lo", [128, NC, B, CH], f32r)

        with ExitStack() as att:
            h_t = sb("h_t", [128, B // 2, NTOK], into=att)
            q_stack = sb("q_stack", [128, HEADS * D], f32r, into=att)
            e_t = sb("e_t", [128, HP, D], into=att)
            s_f = sb("s_f", [128, GB, CH], into=att)
            s_hl = sb("s_hl", [128, 2, GB, CH], f32r, into=att)
            s_lh = sb("s_lh", [128, 2, GB, CH], f32r, into=att)
            s_tok = sb("s_tok", [128, 2, GB, 2, D], into=att)
            with ExitStack() as prep:
                wg = sb("wg", [GF, D, C], into=prep)
                nat = sb("nat", [128, HEADS * D], into=prep)
                nat2 = sb("nat2", [128, HEADS * D], into=prep)
                split_hi = sb("split_hi", [128, HEADS * D], f32r, into=prep)
                w2_diag = sb("w2_diag", [128, EP, 128], into=prep)
                a_w = sb("a_w", [128, 2, QS, D], into=prep)
                a_pad = sb("a_pad", [128, D], into=prep)
                x_edge = sb("x_edge", [128, B, V], into=prep)
                dft_sb = sb("dft_sb", [GF, 2, 2 * QS], into=prep)
                e_nat = sb("e_nat", [D, HP, 2 * D], into=prep)
            q_hi = sb("q_hi", [128, 2, HP, GB, CH], f32r, into=att)
            q_lh = sb("q_lh", [128, 2, HP, GB, CH], f32r, into=att)
            q_hl = sb("q_hl", [128, 2, HP, GB, CH], f32r, into=att)
            o_sb = sb("o_sb", [128, 2, 2, HP, CH], into=att)
            w_t = sb("w_t", [128, HP, GB, CH], into=att)
            r_t = sb("r_t", [128, GB, CH], into=att)
            g_sum = sb("g_sum", [128, B, D], into=att)
            g_hi = sb("g_hi", [128, B, 128], f32r, into=att)
            g_hl = sb("g_hl", [128, B, 128], f32r, into=att)
            g_lh = sb("g_lh", [128, B, 128], f32r, into=att)

        with ExitStack() as ffn:
            sel_sb = sb("sel_sb", [GS, EP * 128], into=ffn)
            sel_r = sb("sel_r", [GS, EP * 128], f32r, into=ffn)
            wo_pair = sb("wo_pair", [128, EP, D], into=ffn)
            w_bc = sb("w_bc", [128, EP, NTOK], into=ffn)
            feat_t = sb("feat_t", [D, NTOK], into=ffn)
            logit = sb("logit", [128, NC, EXP], into=ffn)
            gate = sb("gate", [128, NC, EXP], into=ffn)
            red = sb("red", [128, 3, NC], into=ffn)
            gate_t = sb("gate_t", [EXP, NTOK], into=ffn)
            gate_hl = sb("gate_hl", [GS, NTOK], f32r, into=ffn)
            wbo = sb("wbo", [128, NC, D], into=ffn)
            h2r = sb("h2r", [128, 2, GT], into=ffn)
            h1 = sb("h1", [128, 2, GT], into=ffn)
            h1_hi = sb("h1_hi", [128, 2, EP, GT], f32r, into=ffn)
            h1_lo = sb("h1_lo", [128, 2, EP, GT], f32r, into=ffn)
            y_t = sb("y_t", [128, GT], into=ffn)
            h2w = sb("h2w", [128, 2, EP, GT], into=ffn)
            o_ln = sb("o_ln", [128, 2, GB, D], into=ffn)

        bank = [ctx.enter_context(nc.psum_tensor(f"bank{i}", [128, 512], f32)) for i in range(8)]

        def sems(names):
            return [sem(n) for n in names.split()]

        x_loaded = [[sem(f"x_loaded{i}_{part}") for part in range(2)] for i in range(4)]
        edge_loaded, wg_loaded, dft_loaded, const_loaded, q_loaded, e_loaded, w1_loaded = sems(
            "edge_loaded wg_loaded dft_loaded const_loaded q_loaded e_loaded w1_loaded")
        par_loaded, w2_loaded, small_loaded, sel_loaded = sems("par_loaded w2_loaded small_loaded sel_loaded")
        stored = [sem(f"stored{i}") for i in range(2)]
        w2_zeroed, fills, g_zeroed = sems("w2_zeroed fills g_zeroed")
        a_mm, a_ready, e_t_mm, e_t_ready, par_mm, par_ready = sems("a_mm a_ready e_t_mm e_t_ready par_mm par_ready")
        qs_hi_done, qs_top_done, qs_ready, ws_hi_done, ws_ready, w2_split = sems(
            "qs_hi_done qs_top_done qs_ready ws_hi_done ws_ready w2_split")
        bn_step, bn_sqrt, bn_ready = sems("bn_step bn_sqrt bn_ready")
        tok_mm, ht_act, ht_dve = sems("tok_mm ht_act ht_dve")
        sf_done, sh_done, sl_done, st_mm, st_done = sems("sf_done sh_done sl_done st_mm st_done")
        q_mm, qh_done, ql_done, qx_done = sems("q_mm qh_done ql_done qx_done")
        score_mm, o_done, w_mm, wt_done = sems("score_mm o_done w_mm wt_done")
        g_mm, gsum_done, gh_done, gl_done = sems("g_mm gsum_done gh_done gl_done")
        r_mm, r_done, rs_done, fold_mm = sems("r_mm r_done rs_done fold_mm")
        ln_sum, ln_mean, ln_xm, ln_sq, ln_var, ln_std, ln_rstd = sems(
            "ln_sum ln_mean ln_xm ln_sq ln_var ln_std ln_rstd")
        xs_done, x1_done, feat_part, feat_done, xt_mm, xth_done, xtl_done = sems(
            "xs_done x1_done feat_part feat_done xt_mm xth_done xtl_done")
        ft_mm, ft_done, lg_mm, soft, gate_exp = sems("ft_mm ft_done lg_mm soft gate_exp")
        gate_zeroed, gt_mm, gt_high, gate_split, gt_done, sel_ready, wb_mm, wb_done, wbo_mm, wbo_done, x1b_done = sems(
            "gate_zeroed gt_mm gt_high gate_split gt_done sel_ready wb_mm wb_done wbo_mm wbo_done x1b_done")
        z1_mm, h1_done, h1h_done, h1l_done, z2_mm, h2r_done, h2w_done, y_mm, yt_done, yfold_mm = sems(
            "z1_mm h1_done h1h_done h1l_done z2_mm h2r_done h2w_done y_mm yt_done yfold_mm")
        o_y, o_sum, o_mean, o_xm, o_sq, o_var, o_std, o_rstd, o_ready = sems(
            "o_y o_sum o_mean o_xm o_sq o_var o_std o_rstd o_ready")

        def group(ap, bh, c):
            return ap[:, bass.ds(c, 1), GB * bh:GB * bh + GB, :].rearrange("p a b n -> p (a b) n")

        def per_token(ap):
            return ap.unsqueeze(2).broadcast_to((128, GB, D))

        def bank3(i, a):
            return bank[i][:, :].rearrange("p (a b) -> p a b", a=a)

        slots = [xring[:, s, :, :].rearrange("p m (s v) -> p m s v", s=QS) for s in range(4)]
        a_bank, par_bank, e_t_bank, tok_bank = (4, 5), 5, 6, ((0, 1), (2, 3))
        score_bank, w_bank, r_bank = (0, 1, 2, 3), 5, 6
        z1_bank, z2_bank, yt_bank, y_bank = (0, 1), (2, 3), 4, 5
        feat_bank, logit_bank, gate_bank = (2, 3), 5, (6, 7)
        TOK_TURN, Q_TURN, G_TURN, X_TURN, TURNS = 0, 1, 5, 6, 7

        def turn_bank(bh, turn):
            return (4, 7)[(bh * TURNS + turn) % 2]

        block = ctx.enter_context(nc.Block())

        @block.sync
        def _(sp):
            with nc.allow_non_contiguous_dma(reason="64-channel rows of the tokenizer weight"):
                sp.dma_start(wg[:, :, :], tok_w.rearrange("o (g c) -> g o c", c=C)).then_inc(wg_loaded, 16)
            sp.dma_start(dft_sb[:, :, :], dft).then_inc(dft_loaded, 16)

            parts = (slice(0, NPATCH // 2 + 1), slice(NPATCH // 2 + 1, NPATCH))
            for p in range(B // 2):
                if p >= 2:
                    sp.wait_ge(tok_mm, 4 * (p - 1))
                for part, blocks in enumerate(parts):
                    for b in (2 * p, 2 * p + 1):
                        src = x[b].rearrange("c (m h s) v -> h c m (s v)", h=2, s=QS)
                        for half in range(2):
                            sp.dma_start(xring[64 * half:64 * half + 64, b % 4, blocks, :],
                                         src[half][:, blocks, :]).then_inc(x_loaded[b % 4][part], 16)
                    if p == 0 and part == 0:
                        for half in range(2):
                            sp.dma_start(x_edge[64 * half:64 * half + 64, :, :],
                                         x[:, :, T - 1, :].rearrange("b c v -> c b v")).then_inc(edge_loaded, 16)

            sp.wait_ge(rs_done, NG)
            sp.dma_start(sel_sb[:, :], sel_in).then_inc(sel_loaded, 16)
            sp.dma_start(wo_pair[:, :, :], wo.rearrange("(ep e2) h d -> (e2 h) ep d", e2=2)).then_inc(sel_loaded, 16)

            out_v = out.rearrange("b (c p) d -> p c b d", p=CH)

            def store(m, c, bh):
                sp.wait_ge(o_ready, m + 1)
                sp.dma_start(group(out_v, bh, c), o_ln[:, bh, :, :]).then_inc(stored[bh], 16)

            with sp.Fori(0, NC) as c:
                for bh in range(2):
                    store(2 * c + bh, c, bh)
            for bh in range(2):
                sp.wait_ge(stored[bh], 16 * NC)

        @block.gpsimd
        def _(pool):
            nc.gpsimd.memset(w2_diag[:, :, :], 0.0).then_inc(w2_zeroed, 1)
            nc.gpsimd.memset(eps_ln[:, :], LN_EPS).then_inc(fills, 1)
            nc.gpsimd.memset(eps_bn[:, :], BN_EPS).then_inc(fills, 1)
            nc.gpsimd.memset(g_sum[:, :, :], 0.0).then_inc(g_zeroed, 1)
            for g in (g_hi, g_hl, g_lh):
                nc.gpsimd.memset(g[:, :, :].bitcast(f32), 0.0).then_inc(g_zeroed, 1)
            pool.wait_ge(g_zeroed, 4)
            nc.gpsimd.memset(par[:, 0, :], 0.0).then_inc(xtl_done, 1)

            def s_low(m, bh, own):
                pool.wait_ge(sh_done, 2 * m + 2)
                pool.wait_ge(*own)
                nc.gpsimd.tensor_tensor(s_hl[64:128, bh, :, :], s_f[64:128, :, :], s_lh[64:128, bh, :, :],
                                        ALU.subtract).then_inc(sl_done, 1)
                pool.wait_ge(sl_done, 2 * m + 1)
                nc.gpsimd.tensor_tensor(s_lh[0:64, bh, :, :], s_f[0:64, :, :], s_hl[0:64, bh, :, :],
                                        ALU.subtract).then_inc(sl_done, 1)

            def g_low(m, bh, own):
                bs = slice(GB * bh, GB * bh + GB)
                pool.wait_ge(gh_done, 4 * m + 4)
                pool.wait_ge(*own)
                nc.gpsimd.tensor_tensor(g_hl[64:128, bs, 0:64], g_sum[64:128, bs, :], g_hi[64:128, bs, 64:128],
                                        ALU.subtract).then_inc(gl_done, 1)
                pool.wait_ge(gl_done, 2 * m + 1)
                nc.gpsimd.tensor_tensor(g_lh[0:64, bs, 64:128], g_sum[0:64, bs, :], g_hi[0:64, bs, 0:64],
                                        ALU.subtract).then_inc(gl_done, 1)

            def x1_rows(m, own, free):
                pool.wait_ge(ln_rstd, m + 1)
                if own:
                    pool.wait_ge(*own)
                if free:
                    pool.wait_ge(x1_done, m)
                    pool.wait_ge(xt_mm, m)
                    pool.wait_ge(feat_done, m)
                nc.gpsimd.tensor_tensor(xs[:, :, :, :], xm_ln[:, :, :].unsqueeze(2).broadcast_to((128, GB, 2, D)),
                                        rstd_ln[:, :].unsqueeze(2).unsqueeze(3).broadcast_to((128, GB, 2, D)),
                                        ALU.mult).then_inc(xs_done, 1)

            def step(c, bh, kind):
                m = 2 * c + bh
                split = not (kind == "first" and bh == 0) and not (kind == "last" and bh == 1)
                if kind != "first":
                    x1_rows(m - 2, (gl_done, 2 * m - 2), kind != "second" or bh == 1)
                own = (xs_done, m - 1) if kind != "first" else (sl_done, 2 * m + 4)
                if kind != "last":
                    s_low(m + 2, bh, own)
                    own = (sl_done, 2 * m + 6)
                if split:
                    g_low(m - 1, 1 - bh, own)

            s_low(0, 0, (xtl_done, 1))
            for bh in range(2):
                step(0, bh, "first")
            for bh in range(2):
                step(1, bh, "second")
            with pool.Fori(2, NC - 1) as c:
                for bh in range(2):
                    step(c, bh, "mid")
            for bh in range(2):
                step(NC - 1, bh, "last")

            def hidden1_low(m, bh, ep):
                pool.wait_ge(h1h_done, 4 * m + ep + 1)
                nc.gpsimd.tensor_tensor(h1_lo[:, bh, ep, :], h1[:, ep % 2, :], h1_hi[:, bh, ep, :],
                                        ALU.subtract).then_inc(h1l_done, 1)

            def add_bias(c, bh):
                rows = group(x1, bh, c)
                nc.gpsimd.tensor_tensor(rows, rows, wbo[:, bass.ds(c, 1), :].broadcast_to((128, GB, D)),
                                        ALU.add).then_inc(x1b_done, 1)

            x1_rows(NG - 2, None, True)
            pool.wait_ge(rs_done, NG)
            pool.wait_ge(xs_done, NG - 1)
            nc.gpsimd.memset(gate_hl[:, :].bitcast(f32), 0.0).then_inc(gate_zeroed, 1)
            pool.wait_ge(gate_zeroed, 1)
            hidden1_low(0, 0, 0)
            x1_rows(NG - 1, None, True)
            for ep in range(1, EP):
                hidden1_low(0, 0, ep)
            for ep in range(EP):
                hidden1_low(1, 1, ep)
            pool.wait_ge(x1_done, NG)
            pool.wait_ge(wbo_done, 1)
            add_bias(0, 0)
            add_bias(0, 1)
            with pool.Fori(1, NC) as c:
                for bh in range(2):
                    for ep in range(EP):
                        hidden1_low(2 * c + bh, bh, ep)
                    add_bias(c, bh)

        @block.scalar
        def _(act):
            act.dma_start(ident[:, :], ident_in).then_inc(const_loaded, 16)
            act.dma_start(mask[:, :], mask_in).then_inc(const_loaded, 16)
            act.dma_start(fold[:, :], fold_in).then_inc(const_loaded, 16)
            for h2 in range(2):
                src = att_e[HP * h2:HP * h2 + HP].rearrange("hp i j -> i hp j")
                act.dma_start(e_nat[:, :, D * h2:D * h2 + D], src).then_inc(e_loaded, 16)
            nat_v = nat[:, :].rearrange("p (hp h2 j) -> p hp h2 j", hp=HP, h2=2)
            for half in range(2):
                rows = slice(64 * half, 64 * half + 64)
                for h2 in range(2):
                    act.dma_start(nat_v[rows, :, h2, :],
                                  att_q[HP * h2:HP * h2 + HP].rearrange("hp i j -> i hp j")).then_inc(q_loaded, 16)
                act.dma_start(nat2[rows, :].rearrange("p (e h) -> p e h", e=EXP),
                              w1.rearrange("e d h -> d e h")).then_inc(w1_loaded, 16)
            for n, p in enumerate((b1, g1, be1, m1, v1, b2, g2, be2, m2, v2)):
                act.dma_start(par_rows[EP * n:EP * n + EP, :],
                              p.rearrange("(ep e2) h -> ep (e2 h)", e2=2)).then_inc(par_loaded, 16)
            act.wait_ge(w2_zeroed, 1)
            w2_v = w2.rearrange("(ep e2) h k -> e2 h ep k", e2=2)
            for e2 in range(2):
                blk = slice(64 * e2, 64 * e2 + 64)
                act.dma_start(w2_diag[blk, :, blk], w2_v[e2]).then_inc(w2_loaded, 16)
            act.dma_start(wr_sb[:, :], wr).then_inc(small_loaded, 16)
            act.dma_start(br_sb[:, :], br.partition_broadcast(128)).then_inc(small_loaded, 16)
            act.dma_start(bo_sb[:, :], bo).then_inc(small_loaded, 16)

            act.wait_ge(q_loaded, 64)
            nc.scalar.activation(split_hi[:, :], nat[:, :], ACT.Copy).then_inc(qs_hi_done, 1)
            nc.scalar.activation(q_stack[0:64, :], nat[0:64, :], ACT.Copy).then_inc(qs_top_done, 1)
            act.wait_ge(w1_loaded, 32)
            act.wait_ge(qs_ready, 1)
            nc.scalar.activation(split_hi[:, :], nat2[:, :], ACT.Copy).then_inc(ws_hi_done, 1)
            nc.scalar.activation(w1_stack[0:64, :], nat2[0:64, :], ACT.Copy).then_inc(ws_hi_done, 1)
            act.wait_ge(w2_loaded, 32)
            nc.scalar.activation(w2_hi[:, :, :], w2_diag[:, :, :], ACT.Copy).then_inc(w2_split, 1)
            def s_high(m, bh, free):
                act.wait_ge(sf_done, m + 1)
                if free:
                    act.wait_ge(score_mm, 8 * m - 8)
                nc.scalar.activation(s_hl[0:64, bh, :, :], s_f[0:64, :, :], ACT.Copy).then_inc(sh_done, 1)
                nc.scalar.activation(s_lh[64:128, bh, :, :], s_f[64:128, :, :], ACT.Copy).then_inc(sh_done, 1)

            def q_high(m, bh, hp, free):
                act.wait_ge(q_mm, 4 * m + hp + 1)
                if free and hp == 0:
                    act.wait_ge(w_mm, 4 * m - 4)
                nc.scalar.activation(q_hi[:, bh, hp, :, :], bank3(turn_bank(1 - bh, Q_TURN + hp), GB),
                                     ACT.Copy).then_inc(qh_done, 1)
                act.wait_ge(qh_done, 4 * m + hp + 1)
                nc.scalar.activation(q_lh[64:128, bh, hp, :, :], q_hi[0:64, bh, hp, :, :],
                                     ACT.Copy).then_inc(qx_done, 1)
                nc.scalar.activation(q_hl[0:64, bh, hp, :, :], q_hi[64:128, bh, hp, :, :],
                                     ACT.Copy).then_inc(qx_done, 1)

            def s_tokens(m, bh, free):
                act.wait_ge(st_mm, m + 1)
                if free:
                    act.wait_ge(w_mm, 4 * m - 4)
                    act.wait_ge(g_mm, m - 1)
                tok = bank[turn_bank(1 - bh, TOK_TURN)][:, 0:GB * D].rearrange("p (a b) -> p a b", a=GB)
                nc.scalar.activation(s_tok[:, bh, :, :, :], tok.unsqueeze(2).broadcast_to((128, GB, 2, D)),
                                     ACT.Copy).then_inc(st_done, 1)

            def w_copy(m, k, bh, u, free):
                act.wait_ge(w_mm, k + 1)
                if free and u == 0:
                    act.wait_ge(r_mm, m)
                nc.scalar.activation(w_t[:, :, u, :], bank3(w_bank, HP), ACT.Copy).then_inc(wt_done, 1)

            def r_copy(m):
                act.wait_ge(r_mm, m + 1)
                nc.scalar.activation(r_t[:, :, :], bank3(r_bank, GB), ACT.Copy).then_inc(r_done, 1)

            def keep_x1(m, c, bh):
                act.wait_ge(xs_done, m + 1)
                nc.scalar.activation(group(x1, bh, c), xs[:, :, 0, :], ACT.Copy).then_inc(x1_done, 1)

            def g_high(m, bh):
                act.wait_ge(gsum_done, m + 1)
                act.wait_ge(w_mm, 4 * m + 4)
                bs, up, dn = slice(GB * bh, GB * bh + GB), slice(0, 64), slice(64, 128)
                for dst, blk in ((g_hi, up), (g_hi, dn), (g_hl, up), (g_lh, dn)):
                    nc.scalar.activation(dst[blk, bs, blk], g_sum[blk, bs, :], ACT.Copy).then_inc(gh_done, 1)

            def x_high(m, c, bh, at):
                act.wait_ge(xt_mm, m + 1)
                nc.scalar.activation(group(x1t_hi, bh, c), bank3(at, GB), ACT.Copy).then_inc(xth_done, 1)

            def ln_square(m, s_xm, s_sq):
                act.wait_ge(s_xm, m + 1)
                nc.scalar.activation(y_ln[:, :, :], xm_ln[:, :, :], ACT.Square).then_inc(s_sq, 1)

            def ln_sqrt(m, s_var, s_std):
                act.wait_ge(s_var, m + 1)
                nc.scalar.activation(std_ln[:, :], var_ln[:, :], ACT.Sqrt, bias=eps_ln[:, :],
                                     scale=1.0 / D).then_inc(s_std, 1)

            def step(c, bh, kind):
                m = 2 * c + bh
                prev = not (kind == "first" and bh == 0)
                ahead = not (kind == "last" and bh == 1)
                late = kind != "first"
                for u in range(GB):
                    k = 4 * m + u
                    if prev and u == 0:
                        r_copy(m - 1)
                    if ahead and u == 0:
                        s_tokens(m + 1, 1 - bh, prev)
                    if late and u == 0:
                        ln_sqrt(m - 2, ln_var, ln_std)
                    if ahead and u < 3 and (prev or u > 0):
                        q_high(m + 1, 1 - bh, (0, 1, 3)[u], prev)
                    if late and u == 3:
                        keep_x1(m - 2, c - 1, bh)
                    w_copy(m, k, bh, u, prev)
                    if not prev and u == 0:
                        q_high(m + 1, 1 - bh, 0, prev)
                    if ahead and u == 1:
                        q_high(m + 1, 1 - bh, 2, prev)
                    if kind != "last" and u == 2:
                        s_high(m + 2, bh, True)
                    if prev and u == 2 and ahead:
                        g_high(m - 1, 1 - bh)
                    if late and u == 3:
                        x_high(m - 2, c - 1, bh, turn_bank(bh, X_TURN))
                    if prev and u == 3:
                        ln_square(m - 1, ln_xm, ln_sq)

            hv = h_t[:, :, :].rearrange("p b (v n) -> p b n v", n=NPATCH)

            def tokens(p, g):
                act.wait_ge(tok_mm, 4 * p + 2 * g + 2)
                nc.scalar.activation(hv[0:64, p, 8 * g:8 * g + 8, :], bank3(tok_bank[p % 2][g], 8)[0:64],
                                     ACT.Copy).then_inc(ht_act, 1)

            for p in range(2):
                for g in range(2):
                    tokens(p, g)
            act.wait_ge(g_zeroed, 4)
            s_high(0, 0, False)
            act.wait_ge(par_ready, 1)
            act.wait_ge(fills, 2)
            for n in range(2):
                nc.scalar.activation(bn_tmp[:, n, :], par[:, 5 * n + 4, :], ACT.Sqrt,
                                     bias=eps_bn[:, :]).then_inc(bn_sqrt, 1)
            tokens(2, 0)
            s_tokens(0, 0, False)
            q_high(0, 0, 0, False)
            q_high(0, 0, 1, False)
            tokens(2, 1)
            q_high(0, 0, 2, False)
            q_high(0, 0, 3, False)
            tokens(3, 0)
            tokens(3, 1)
            s_high(1, 1, False)
            for bh in range(2):
                step(0, bh, "first")
            with act.Fori(1, NC - 1) as c:
                for bh in range(2):
                    step(c, bh, "mid")
            for bh in range(2):
                step(NC - 1, bh, "last")
            def hidden1(m, ep, free):
                act.wait_ge(z1_mm, 4 * m + ep + 1)
                if free or ep >= 2:
                    act.wait_ge(h1l_done, 4 * m + ep - 1)
                nc.scalar.activation(h1[:, ep % 2, :], bank[z1_bank[ep % 2]][:, :], ACT.Relu,
                                     bias=bn_bias[:, 0, ep:ep + 1],
                                     scale=bn_scale[:, 0, ep:ep + 1]).then_inc(h1_done, 1)

            def features(i, a, b):
                act.wait_ge(ft_mm, b)
                at = CH * (a - i * NC // 2)
                nc.scalar.activation(feat_t[:, CH * a:CH * b], bank[feat_bank[i]][0:D, at:at + CH * (b - a)], ACT.Copy,
                                     scale=1.0 / B).then_inc(ft_done, 1)

            r_copy(NG - 1)
            ln_sqrt(NG - 2, ln_var, ln_std)
            act.wait_ge(bn_ready, 2)
            for ep in range(2):
                hidden1(0, ep, False)
            keep_x1(NG - 2, NC - 1, 0)
            features(0, 0, NC // 2)
            x_high(NG - 2, NC - 1, 0, turn_bank(0, X_TURN))
            ln_square(NG - 1, ln_xm, ln_sq)
            ln_sqrt(NG - 1, ln_var, ln_std)
            hidden1(0, 2, False)
            features(1, NC // 2, NC - 1)
            keep_x1(NG - 1, NC - 1, 1)
            act.wait_ge(sel_loaded, 32)
            nc.scalar.activation(sel_r[:, :], sel_sb[:, :], ACT.Copy).then_inc(sel_ready, 1)
            features(1, NC - 1, NC)
            x_high(NG - 1, NC - 1, 1, turn_bank(1, X_TURN))

            act.wait_ge(soft, 3)
            nc.scalar.activation(gate[:, :, :], logit[:, :, :], ACT.Exp).then_inc(gate_exp, 1)
            nc.scalar.activation(std_ln[:, 0:1], eps_ln[:, :], ACT.Sqrt)

            act.wait_ge(gate_zeroed, 1)
            halves = [slice(GT * i, GT * i + GT) for i in range(2)]
            for i in range(2):
                act.wait_ge(gt_mm, 4 * i + 4)
                nc.scalar.activation(gate_hl[0:EXP, halves[i]], bank[feat_bank[i]][0:EXP, :],
                                     ACT.Copy).then_inc(gt_high, 1)

            def gate_rows(i):
                act.wait_ge(wb_mm, i + 1)
                nc.scalar.activation(w_bc[:, i % EP, GT * (i // EP):GT * (i // EP) + GT], bank[gate_bank[i % 2]][:, :],
                                     ACT.Copy).then_inc(wb_done, 1)

            gate_rows(0)
            for i in range(2):
                act.wait_ge(gate_split, i + 1)
                nc.scalar.activation(gate_t[:, halves[i]], bank[feat_bank[i]][0:EXP, :], ACT.Copy).then_inc(gt_done, 1)
                gate_rows(1 + i)
            gate_rows(3)
            hidden1(0, 3, False)

            def hidden2(m, ep, free):
                act.wait_ge(z2_mm, 4 * m + ep + 1)
                if free or ep >= 2:
                    act.wait_ge(h2w_done, 4 * m + ep - 1)
                nc.scalar.activation(h2r[:, ep % 2, :], bank[z2_bank[ep % 2]][:, :], ACT.Relu,
                                     bias=bn_bias[:, 1, ep:ep + 1],
                                     scale=bn_scale[:, 1, ep:ep + 1]).then_inc(h2r_done, 1)

            def y_copy(m):
                act.wait_ge(y_mm, m + 1)
                nc.scalar.activation(y_t[:, :], bank[yt_bank][:, :], ACT.Copy).then_inc(yt_done, 1)

            def expert_step(c, bh, kind):
                m = 2 * c + bh
                prev = not (kind == "first" and bh == 0)
                for ep in range(EP):
                    if prev and ep == 2:
                        y_copy(m - 1)
                    if not (kind == "last" and bh == 1):
                        hidden1(m + 1, ep, True)
                    if kind != "first" and ep == 2:
                        ln_square(m - 2, o_xm, o_sq)
                    hidden2(m, ep, prev)
                    if not prev:
                        gate_rows(EP + ep)
                        if ep == EP - 1:
                            act.wait_ge(wbo_mm, NC)
                            nc.scalar.activation(wbo[:, :, :], bank3(y_bank, NC), ACT.Copy).then_inc(wbo_done, 1)
                    if kind != "first" and ep == 3:
                        ln_sqrt(m - 2, o_var, o_std)

            for bh in range(2):
                expert_step(0, bh, "first")
            with act.Fori(1, NC - 1) as c:
                for bh in range(2):
                    expert_step(c, bh, "mid")
            for bh in range(2):
                expert_step(NC - 1, bh, "last")
            ln_square(NG - 2, o_xm, o_sq)
            ln_sqrt(NG - 2, o_var, o_std)
            y_copy(NG - 1)
            ln_square(NG - 1, o_xm, o_sq)
            ln_sqrt(NG - 1, o_var, o_std)

        @block.vector
        def _(dve):
            dve.wait_ge(a_mm, 1)
            for i in range(2):
                src = bank[a_bank[i]][0:64, :].rearrange("p (o h k) -> p h k o", h=2, k=2 * QS)
                for half in range(2):
                    at = a_w[64 * half:64 * half + 64, :, :, D // 2 * i:D // 2 * i + D // 2]
                    nc.vector.tensor_copy(at.rearrange("p q s o -> p (q s) o"), src[:, half]).then_inc(a_ready, 1)
            dve.wait_ge(a_ready, 4)
            nc.vector.tensor_reduce(a_pad[:, :], a_w[:, 1, :, :].rearrange("p s o -> p o s"), AX.X,
                                    ALU.add).then_inc(a_ready, 1)
            dve.wait_ge(q_loaded, 64)
            dve.wait_ge(qs_hi_done, 1)
            nc.vector.tensor_tensor(q_stack[64:128, :], nat[64:128, :], split_hi[64:128, :],
                                    ALU.subtract).then_inc(qs_ready, 1)
            dve.wait_ge(w1_loaded, 32)
            dve.wait_ge(ws_hi_done, 1)
            nc.vector.tensor_tensor(w1_stack[64:128, :], nat2[64:128, :], split_hi[64:128, :],
                                    ALU.subtract).then_inc(ws_ready, 1)
            dve.wait_ge(w2_split, 1)
            dve.wait_ge(w2_loaded, 32)
            nc.vector.tensor_tensor(w2_lo[:, :, :], w2_diag[:, :, :], w2_hi[:, :, :],
                                    ALU.subtract).then_inc(w2_split, 1)
            def s_stage(m, c, bh, free):
                if free:
                    dve.wait_ge(st_mm, m)
                    dve.wait_ge(sl_done, 2 * m)
                for j in range(2):
                    src = h_t[64 * j:64 * j + 64, 2 * bh:2 * bh + 2, bass.ds(c * CH, CH)]
                    for half in range(2):
                        dst = s_f[64 * half:64 * half + 64, :, :].rearrange("p (a j) t -> p j a t", j=2)
                        last = nc.vector.tensor_copy(dst[:, j], src)
                last.then_inc(sf_done, 1)

            def q_low(m, bh, hp):
                dve.wait_ge(qh_done, 4 * m + hp + 1)
                src = bank3(turn_bank(1 - bh, Q_TURN + hp), GB)
                for dst, half in ((q_lh, slice(0, 64)), (q_hl, slice(64, 128))):
                    last = nc.vector.tensor_tensor(dst[half, bh, hp, :, :], src[half], q_hi[half, bh, hp, :, :],
                                                   ALU.subtract)
                last.then_inc(ql_done, 1)

            def mask_scores(k, par_k, free):
                if free:
                    dve.wait_ge(w_mm, k - 1)
                for h2 in range(2):
                    dve.wait_ge(score_mm, 2 * k + h2 + 1)
                    nc.vector.tensor_tensor(o_sb[:, par_k, h2, :, :], bank3(score_bank[2 * par_k + h2], HP),
                                            mask[:, :].unsqueeze(1).broadcast_to((128, HP, CH)),
                                            ALU.mult).then_inc(o_done, 1)

            def ln_first(m, s, y, free):
                nc.vector.tensor_reduce(sum_ln[:, :], y, AX.X, ALU.add).then_inc(s["sum"], 1)
                dve.wait_ge(s["sum"], m + 1)
                nc.vector.tensor_scalar(mean_ln[:, :], sum_ln[:, :], 1.0 / D, None, ALU.mult).then_inc(s["mean"], 1)
                dve.wait_ge(s["mean"], m + 1)
                if free:
                    dve.wait_ge(xs_done, m)
                nc.vector.tensor_tensor(xm_ln[:, :, :], y, per_token(mean_ln[:, :]),
                                        ALU.subtract).then_inc(s["xm"], 1)

            def ln_var_sum(m, s):
                dve.wait_ge(s["sq"], m + 1)
                nc.vector.tensor_reduce(var_ln[:, :], y_ln[:, :, :], AX.X, ALU.add).then_inc(s["var"], 1)

            def ln_reciprocal(m, s):
                dve.wait_ge(s["std"], m + 1)
                nc.vector.reciprocal(rstd_ln[:, :], std_ln[:, :]).then_inc(s["rstd"], 1)

            ln1 = dict(sum=ln_sum, mean=ln_mean, xm=ln_xm, sq=ln_sq, var=ln_var, std=ln_std, rstd=ln_rstd)
            ln2 = dict(sum=o_sum, mean=o_mean, xm=o_xm, sq=o_sq, var=o_var, std=o_std, rstd=o_rstd)

            def add_tokens(m, c, bh):
                dve.wait_ge(r_done, m + 1)
                for j in range(2):
                    at = r_t[64 * j:64 * j + 64, :, :].rearrange("p (a j) t -> p j a t", j=2)[:, j]
                    last = nc.vector.tensor_tensor(at, at, h_t[64 * j:64 * j + 64, 2 * bh:2 * bh + 2,
                                                               bass.ds(c * CH, CH)], ALU.add)
                last.then_inc(rs_done, 1)

            def center(m, free):
                dve.wait_ge(fold_mm, m + 1)
                ln_first(m, ln1, bank[r_bank][:, 0:GB * D].rearrange("p (a b) -> p a b", a=GB), free)

            def g_add(m, bh, free):
                dve.wait_ge(g_mm, m + 1)
                if free:
                    dve.wait_ge(gl_done, 2 * m - 2)
                bs = slice(GB * bh, GB * bh + GB)
                nc.vector.tensor_tensor(g_sum[:, bs, :], g_sum[:, bs, :],
                                        bank[turn_bank(bh, G_TURN)][:, 0:GB * D].rearrange("p (a b) -> p a b", a=GB),
                                        ALU.add).then_inc(gsum_done, 1)

            def feature_sum(m, c, bh):
                dve.wait_ge(xs_done, m + 1)
                rows = xs[:, :, 0, :].rearrange("p b d -> p d b")
                at = feat[:, bass.ds(c, 1), :].rearrange("p a d -> p (a d)")
                if bh == 0:
                    nc.vector.tensor_reduce(at, rows, AX.X, ALU.add).then_inc(feat_done, 1)
                else:
                    nc.vector.tensor_reduce(feat_half[:, :], rows, AX.X, ALU.add).then_inc(feat_part, 1)
                    dve.wait_ge(feat_part, c + 1)
                    nc.vector.tensor_tensor(at, at, feat_half[:, :], ALU.add).then_inc(feat_done, 1)

            def x_low(m, c, bh, at):
                dve.wait_ge(xth_done, m + 1)
                nc.vector.tensor_tensor(group(x1t_lo, bh, c), bank3(at, GB), group(x1t_hi, bh, c),
                                        ALU.subtract).then_inc(xtl_done, 1)

            def step(c, bh, kind):
                m = 2 * c + bh
                prev = not (kind == "first" and bh == 0)
                ahead = not (kind == "last" and bh == 1)
                late = kind != "first"
                for u in range(GB):
                    k = 4 * m + u
                    if ahead or u < GB - 1:
                        mask_scores(k + 1, (u + 1) % 2, prev or u >= 1)
                    if late and u == 0:
                        ln_var_sum(m - 2, ln1)
                    if prev and u == 0:
                        add_tokens(m - 1, c if bh else c - 1, 1 - bh)
                    if ahead and u < 3:
                        q_low(m + 1, 1 - bh, (0, 1, 3)[u])
                    if late and u == 0:
                        ln_reciprocal(m - 2, ln1)
                    if ahead and u == 1:
                        q_low(m + 1, 1 - bh, 2)
                    if kind != "last" and u == 2:
                        s_stage(m + 2, c + 1, bh, True)
                    if kind != "last" and u == 3:
                        g_add(m, bh, late)
                    if prev and u == 3:
                        center(m - 1, late)
                    if late and u == 3:
                        feature_sum(m - 2, c - 1, bh)
                        x_low(m - 2, c - 1, bh, turn_bank(bh, X_TURN))

            hv = h_t[:, :, :].rearrange("p b (v n) -> p b n v", n=NPATCH)

            def tokens(p, g):
                dve.wait_ge(tok_mm, 4 * p + 2 * g + 2)
                nc.vector.tensor_copy(hv[64:128, p, 8 * g:8 * g + 8, :],
                                      bank3(tok_bank[p % 2][g], 8)[64:128]).then_inc(ht_dve, 1)

            tokens(0, 0)
            tokens(0, 1)
            dve.wait_ge(e_t_mm, 1)
            nc.vector.tensor_copy(e_t[:, :, :], bank[e_t_bank][:, 0:HP * D].rearrange("p (a b) -> p a b",
                                  a=HP)).then_inc(e_t_ready, 1)
            tokens(1, 0)
            tokens(1, 1)
            dve.wait_ge(ht_dve, B // 2)
            dve.wait_ge(ht_act, B // 2)
            s_stage(0, 0, 0, False)
            dve.wait_ge(par_mm, 1)
            dve.wait_ge(xtl_done, 1)
            nc.vector.tensor_copy(par[:, :, :].rearrange("p n e -> p (n e)"), bank[par_bank][:,
                                  0:NPAR * EP]).then_inc(par_ready, 1)
            dve.wait_ge(bn_sqrt, 2)
            dve.wait_ge(par_ready, 1)
            nc.vector.reciprocal(bn_scale[:, :, :], bn_tmp[:, :, :]).then_inc(bn_step, 1)
            for n in range(2):
                dve.wait_ge(bn_step, 4 * n + 1)
                nc.vector.tensor_tensor(bn_scale[:, n, :], bn_scale[:, n, :], par[:, 5 * n + 1, :],
                                        ALU.mult).then_inc(bn_step, 1)
                nc.vector.tensor_tensor(bn_bias[:, n, :], par[:, 5 * n, :], par[:, 5 * n + 3, :],
                                        ALU.subtract).then_inc(bn_step, 1)
                dve.wait_ge(bn_step, 4 * n + 3)
                nc.vector.tensor_tensor(bn_bias[:, n, :], bn_bias[:, n, :], bn_scale[:, n, :],
                                        ALU.mult).then_inc(bn_step, 1)
                dve.wait_ge(bn_step, 4 * n + 4)
                nc.vector.tensor_tensor(bn_bias[:, n, :], bn_bias[:, n, :], par[:, 5 * n + 2, :],
                                        ALU.add).then_inc(bn_step, 1)
            dve.wait_ge(bn_step, 9)
            nc.vector.tensor_copy(bn_tmp[:, 0, :], bn_bias[:, 0, :]).then_inc(bn_ready, 2)

            dve.wait_ge(const_loaded, 48)
            tokens(2, 0)
            q_low(0, 0, 0)
            q_low(0, 0, 1)
            tokens(2, 1)
            q_low(0, 0, 2)
            q_low(0, 0, 3)
            tokens(3, 0)
            mask_scores(0, 0, False)
            tokens(3, 1)
            dve.wait_ge(ht_dve, B)
            dve.wait_ge(ht_act, B)
            s_stage(1, 0, 1, True)
            dve.wait_ge(sh_done, 4)
            nc.vector.tensor_tensor(s_hl[64:128, 1, :, :], s_f[64:128, :, :], s_lh[64:128, 1, :, :],
                                    ALU.subtract).then_inc(sl_done, 1)
            nc.vector.tensor_tensor(s_lh[0:64, 1, :, :], s_f[0:64, :, :], s_hl[0:64, 1, :, :],
                                    ALU.subtract).then_inc(sl_done, 1)
            for bh in range(2):
                step(0, bh, "first")
            with dve.Fori(1, NC - 1) as c:
                for bh in range(2):
                    step(c, bh, "mid")
            for bh in range(2):
                step(NC - 1, bh, "last")
            def hidden1_high(m, bh, ep, free):
                dve.wait_ge(h1_done, 4 * m + ep + 1)
                if free and ep == 0:
                    dve.wait_ge(z2_mm, 4 * m - 4)
                nc.vector.tensor_copy(h1_hi[:, bh, ep, :], h1[:, ep % 2, :]).then_inc(h1h_done, 1)

            ln_var_sum(NG - 2, ln1)
            add_tokens(NG - 1, NC - 1, 1)
            ln_reciprocal(NG - 2, ln1)
            hidden1_high(0, 0, 0, False)
            hidden1_high(0, 0, 1, False)
            center(NG - 1, True)
            feature_sum(NG - 2, NC - 1, 0)
            ln_var_sum(NG - 1, ln1)
            ln_reciprocal(NG - 1, ln1)
            x_low(NG - 2, NC - 1, 0, turn_bank(0, X_TURN))
            hidden1_high(0, 0, 2, False)
            feature_sum(NG - 1, NC - 1, 1)

            dve.wait_ge(lg_mm, NC)
            dve.wait_ge(small_loaded, 48)
            ps_lg = bank[logit_bank][:, 0:NC * EXP].rearrange("p (c e) -> p c e", e=EXP)
            nc.vector.tensor_tensor(logit[:, :, :], ps_lg, br_sb[:, :].unsqueeze(1).broadcast_to((128, NC, EXP)),
                                    ALU.add).then_inc(soft, 1)
            dve.wait_ge(soft, 1)
            nc.vector.tensor_reduce(red[:, 0, :], logit[:, :, :], AX.X, ALU.max).then_inc(soft, 1)
            dve.wait_ge(soft, 2)
            nc.vector.tensor_tensor(logit[:, :, :], logit[:, :, :],
                                    red[:, 0, :].unsqueeze(2).broadcast_to((128, NC, EXP)), ALU.subtract).then_inc(soft, 1)
            x_low(NG - 1, NC - 1, 1, turn_bank(1, X_TURN))
            dve.wait_ge(gate_exp, 1)
            nc.vector.tensor_reduce(red[:, 1, :], gate[:, :, :], AX.X, ALU.add).then_inc(soft, 1)
            dve.wait_ge(soft, 4)
            nc.vector.reciprocal(red[:, 2, :], red[:, 1, :]).then_inc(soft, 1)
            dve.wait_ge(soft, 5)
            nc.vector.tensor_tensor(gate[:, :, :], gate[:, :, :],
                                    red[:, 2, :].unsqueeze(2).broadcast_to((128, NC, EXP)), ALU.mult).then_inc(soft, 1)

            for i in range(2):
                dve.wait_ge(gt_high, i + 1)
                half = slice(GT * i, GT * i + GT)
                nc.vector.tensor_tensor(gate_hl[GS - EXP:GS, half], bank[feat_bank[i]][0:EXP, :], gate_hl[0:EXP, half],
                                        ALU.subtract).then_inc(gate_split, 1)
            hidden1_high(0, 0, 3, False)

            def gate_hidden(m, c, bh, ep, free):
                dve.wait_ge(h2r_done, 4 * m + ep + 1)
                if free and ep == 0:
                    dve.wait_ge(y_mm, m - 1)
                nc.vector.tensor_tensor(
                    h2w[:, bh, ep, :].rearrange("p (b t) -> p b t", b=GB),
                    h2r[:, ep % 2, :].rearrange("p (b t) -> p b t", b=GB),
                    w_bc[:, ep, bass.ds(c * CH, CH)].unsqueeze(1).broadcast_to((128, GB, CH)),
                    ALU.mult).then_inc(h2w_done, 1)

            def out_residual(m, c, bh):
                dve.wait_ge(yfold_mm, m + 1)
                dve.wait_ge(x1b_done, m + 1)
                nc.vector.tensor_tensor(y_ln[:, :, :],
                                        bank[y_bank][:, 0:GB * D].rearrange("p (a b) -> p a b", a=GB),
                                        group(x1, bh, c), ALU.add).then_inc(o_y, 1)

            def out_center(m):
                dve.wait_ge(o_y, m + 1)
                ln_first(m, ln2, y_ln[:, :, :], False)

            def out_scale(m, c, bh, free):
                if free:
                    dve.wait_ge(stored[bh], 16 * c)
                ln_reciprocal(m, ln2)
                dve.wait_ge(o_rstd, m + 1)
                nc.vector.tensor_tensor(o_ln[:, bh, :, :], xm_ln[:, :, :], per_token(rstd_ln[:, :]),
                                        ALU.mult).then_inc(o_ready, 1)

            def expert_step(c, bh, kind):
                m = 2 * c + bh
                late = kind != "first"
                for ep in range(EP):
                    if not (kind == "last" and bh == 1):
                        hidden1_high(m + 1, 1 - bh, ep, late or bh == 1)
                    gate_hidden(m, c, bh, ep, late)
                    if late:
                        if ep == 0:
                            out_residual(m - 2, c - 1, bh)
                            out_center(m - 2)
                        if ep == 2:
                            ln_var_sum(m - 2, ln2)
                        if ep == 3:
                            out_scale(m - 2, c - 1, bh, kind != "second")

            dve.wait_ge(wb_done, EP)
            for bh in range(2):
                expert_step(0, bh, "first")
            dve.wait_ge(wb_done, 2 * EP)
            for bh in range(2):
                expert_step(1, bh, "second")
            with dve.Fori(2, NC - 1) as c:
                for bh in range(2):
                    expert_step(c, bh, "mid")
            for bh in range(2):
                expert_step(NC - 1, bh, "last")
            for m in (NG - 2, NG - 1):
                out_residual(m, NC - 1, m % 2)
                out_center(m)
                ln_var_sum(m, ln2)
                out_scale(m, NC - 1, m % 2, True)

        @block.tensor
        def _(pe):
            def mm(o, lhs_t, rhs, start=True, stop=True):
                return nc.tensor.matmul(o, lhs_t, rhs, start=start, stop=stop, skip_group_check=True)

            pe.wait_ge(wg_loaded, 16)
            pe.wait_ge(dft_loaded, 16)
            for o in range(D):
                at = 4 * QS * (o % (D // 2))
                last = mm(bank[a_bank[2 * o // D]][0:64, at:at + 4 * QS], wg[:, o, :],
                          dft_sb[:, :, :].rearrange("g h k -> g (h k)"))
            last.then_inc(a_mm, 1)

            def tokens(p, g):
                for b in (2 * p, 2 * p + 1):
                    pe.wait_ge(x_loaded[b % 4][g], 32 * (b // 4 + 1))
                if p >= 2:
                    pe.wait_ge(ht_act, 2 * (p - 2) + g + 1)
                    pe.wait_ge(ht_dve, 2 * (p - 2) + g + 1)
                ps = bank3(tok_bank[p % 2][g], 8)
                for q in range(2):
                    n = 8 if q == 0 or g == 0 else 7
                    for s in range(QS):
                        for j in range(2):
                            end = g == 0 and q == 1 and s == QS - 1
                            last = mm(ps[64 * j:64 * j + 64, 0:n, :], a_w[:, q, s, :],
                                      slots[(2 * p + j) % 4][:, 8 * g + q:8 * g + q + n, s, :], start=(q + s == 0),
                                      stop=end)
                            if end:
                                last.then_inc(tok_mm, 1)
                if g == 1:
                    if p == 0:
                        pe.wait_ge(edge_loaded, 32)
                    for j in range(2):
                        mm(ps[64 * j:64 * j + 64, 7, :], a_pad[:, :], x_edge[:, 2 * p + j, :],
                           start=False).then_inc(tok_mm, 1)

            def queries(m, bh, hp):
                cols = slice(128 * hp, 128 * hp + 128)
                o = bank[turn_bank(1 - bh, Q_TURN + hp)][:, :]
                mm(o, q_stack[:, cols], s_hl[:, bh, :, :], stop=False)
                mm(o, q_stack[:, cols], s_lh[:, bh, :, :], start=False).then_inc(q_mm, 1)

            def transposes(bh):
                for u in range(GB):
                    last = nc.tensor.transpose(bank[turn_bank(1 - bh, TOK_TURN)][:, D * u:D * u + D], s_f[0:D, u, :],
                                               ident[0:D, 0:D])
                last.then_inc(st_mm, 1)

            def scores(k, bh, u, free):
                for h2, stack, q_stacked in ((0, s_hl, q_lh), (1, s_lh, q_hl)):
                    rows = slice(64 * h2, 64 * h2 + 64)
                    if free:
                        pe.wait_ge(o_done, 2 * k - 3 + h2)
                    o = bank[score_bank[2 * (u % 2) + h2]][:, :]
                    mm(o, stack[rows, bh, u, :], q_hi[rows, bh, :, u, :], stop=False)
                    mm(o, stack[:, bh, u, :], q_stacked[:, bh, :, u, :], start=False).then_inc(score_mm, 1)

            def values(m, k, bh, u, kind):
                if not (kind == "first" and bh == 0 and u == 0):
                    pe.wait_ge(wt_done, k)
                inter = kind != "first"
                if inter:
                    if u == 0:
                        pe.wait_ge(gl_done, 2 * m - 2)
                    b = GB * bh + u
                    mm(bank[w_bank][:, :], g_hi[:, b, :], q_hi[:, bh, :, u, :], stop=False)
                    mm(bank[w_bank][:, :], g_hl[:, b, :], q_lh[:, bh, :, u, :], start=False, stop=False)
                    mm(bank[w_bank][:, :], g_lh[:, b, :], q_hl[:, bh, :, u, :], start=False, stop=False)
                if u == 0:
                    pe.wait_ge(st_done, m + 1)
                for h2 in range(2):
                    pe.wait_ge(o_done, 2 * k + h2 + 1)
                    last = mm(bank[w_bank][64 * h2:64 * h2 + 64, :], s_tok[:, bh, u, 0, :], o_sb[:, u % 2, h2, :, :],
                              start=not inter)
                last.then_inc(w_mm, 1)

            def state(bh):
                for u in range(GB):
                    last = mm(bank[turn_bank(bh, G_TURN)][:, D * u:D * u + D],
                              s_tok[:, bh, u, :, :].rearrange("p r d -> p (r d)"), s_tok[:, bh, u, 0, :])
                last.then_inc(g_mm, 1)

            def outputs(m, bh, free):
                pe.wait_ge(wt_done, 4 * m + 4)
                if free:
                    pe.wait_ge(ln_xm, m)
                for hp in range(HP):
                    half = hp % 2
                    last = mm(bank[r_bank][64 * half:64 * half + 64, :], e_t[:, hp, :], w_t[:, hp, :, :],
                              start=(hp < 2), stop=(hp >= 2))
                last.then_inc(r_mm, 1)

            def fold_rows(at, rows, done):
                for u in range(GB):
                    last = mm(bank[at][:, D * u:D * u + D], rows(u), fold[:, :])
                last.then_inc(done, 1)

            def fold_r(m):
                pe.wait_ge(rs_done, m + 1)
                fold_rows(r_bank, lambda u: r_t[:, u, :], fold_mm)

            def x_transposes(m, at):
                pe.wait_ge(xs_done, m + 1)
                for u in range(GB):
                    last = nc.tensor.transpose(bank[at][:, CH * u:CH * u + CH],
                                               xs[:, u, :, :].rearrange("p r d -> p (r d)"), ident[:, :])
                last.then_inc(xt_mm, 1)

            def step(c, bh, kind):
                m = 2 * c + bh
                prev = not (kind == "first" and bh == 0)
                ahead = not (kind == "last" and bh == 1)
                late = kind != "first"
                for u in range(GB):
                    k = 4 * m + u
                    if ahead or u < GB - 1:
                        if u == GB - 1:
                            pe.wait_ge(ql_done, 4 * m + 8)
                            pe.wait_ge(qx_done, 8 * m + 16)
                        scores(k + 1, bh if u < GB - 1 else 1 - bh, (u + 1) % GB, prev or u >= 1)
                    if ahead and u == 0:
                        pe.wait_ge(sf_done, m + 2)
                        if prev:
                            pe.wait_ge(gsum_done, m)
                    if prev and u == 0:
                        outputs(m - 1, 1 - bh, late)
                    if ahead and u == 0:
                        transposes(1 - bh)
                        if not prev:
                            values(m, k, bh, u, kind)
                        pe.wait_ge(sl_done, 2 * m + 4)
                        if late:
                            pe.wait_ge(xtl_done, m - 1)
                        queries(m + 1, 1 - bh, 0)
                    if ahead and u == 1:
                        pe.wait_ge(st_done, m + 2)
                        queries(m + 1, 1 - bh, 1)
                    if ahead and u == 2:
                        pe.wait_ge(ql_done, 4 * m + 6)
                        queries(m + 1, 1 - bh, 3)
                    if prev or u > 0:
                        values(m, k, bh, u, kind)
                    if ahead and u == 1:
                        pe.wait_ge(ql_done, 4 * m + 5)
                        queries(m + 1, 1 - bh, 2)
                    if prev and u == 1:
                        fold_r(m - 1)
                    if kind != "last" and u == 2:
                        pe.wait_ge(ql_done, 4 * m + 7)
                        state(bh)
                    if late and u == 3:
                        x_transposes(m - 2, turn_bank(bh, X_TURN))

            pe.wait_ge(a_ready, 5)
            tokens(0, 0)
            tokens(0, 1)
            pe.wait_ge(const_loaded, 48)
            pe.wait_ge(e_loaded, 32)
            for hp in range(HP):
                last = nc.tensor.transpose(bank[e_t_bank][:, D * hp:D * hp + D], e_nat[:, hp, :], ident[0:D, 0:D])
            last.then_inc(e_t_mm, 1)
            tokens(1, 0)
            tokens(1, 1)
            pe.wait_ge(par_loaded, 16 * NPAR)
            nc.tensor.transpose(bank[par_bank][:, 0:NPAR * EP], par_rows[:, :], ident[0:NPAR * EP,
                                0:NPAR * EP]).then_inc(par_mm, 1)
            tokens(2, 0)
            pe.wait_ge(sf_done, 1)
            transposes(0)
            pe.wait_ge(qs_ready, 1)
            pe.wait_ge(qs_top_done, 1)
            pe.wait_ge(sl_done, 2)
            queries(0, 0, 0)
            pe.wait_ge(st_done, 1)
            queries(0, 0, 1)
            tokens(2, 1)
            for hp in range(2, HP):
                pe.wait_ge(ql_done, hp - 1)
                queries(0, 0, hp)
            tokens(3, 0)
            pe.wait_ge(ql_done, HP)
            pe.wait_ge(qx_done, 2 * HP)
            pe.wait_ge(ht_act, B - 2)
            pe.wait_ge(ht_dve, B - 2)
            scores(0, 0, 0, False)
            tokens(3, 1)
            pe.wait_ge(ht_act, B)
            pe.wait_ge(ht_dve, B)
            pe.wait_ge(e_t_ready, 1)
            pe.wait_ge(par_ready, 1)
            for bh in range(2):
                step(0, bh, "first")
            with pe.Fori(1, NC - 1) as c:
                for bh in range(2):
                    step(c, bh, "mid")
            for bh in range(2):
                step(NC - 1, bh, "last")
            def layer1(m, c, bh, ep, free):
                if free or ep >= 2:
                    pe.wait_ge(h1_done, 4 * m + ep - 1)
                o = bank[z1_bank[ep % 2]][:, :]
                cols = slice(128 * ep, 128 * ep + 128)
                mm(o, w1_stack[:, cols], group(x1t_hi, bh, c), stop=False)
                mm(o, w1_stack[:, cols], group(x1t_lo, bh, c), start=False).then_inc(z1_mm, 1)

            def features(a, b):
                pe.wait_ge(feat_done, 2 * b)
                for c in range(a, b):
                    at = CH * (c % (NC // 2))
                    nc.tensor.transpose(bank[feat_bank[2 * c // NC]][0:D, at:at + CH], feat[:, c, :],
                                        ident[:, :]).then_inc(ft_mm, 1)

            def logits(a, b, done):
                pe.wait_ge(ft_done, done)
                for c in range(a, b):
                    mm(bank[logit_bank][:, EXP * c:EXP * c + EXP], feat_t[:, CH * c:CH * c + CH],
                       wr_sb[:, :]).then_inc(lg_mm, 1)

            outputs(NG - 1, 1, True)
            pe.wait_ge(ws_ready, 1)
            pe.wait_ge(ws_hi_done, 2)
            for ep in range(2):
                layer1(0, 0, 0, ep, False)
            fold_r(NG - 1)
            features(0, NC // 2)
            pe.wait_ge(xtl_done, NG - 2)
            x_transposes(NG - 2, turn_bank(0, X_TURN))
            pe.wait_ge(small_loaded, 48)
            logits(0, NC // 2, 1)
            for ep in range(2, EP):
                layer1(0, 0, 0, ep, False)
            features(NC // 2, NC - 1)
            logits(NC // 2, NC - 1, 2)
            features(NC - 1, NC)
            pe.wait_ge(xtl_done, NG - 1)
            x_transposes(NG - 1, turn_bank(1, X_TURN))
            logits(NC - 1, NC, 3)

            pe.wait_ge(soft, 6)
            for c in range(NC):
                at = CH * (c % (NC // 2))
                nc.tensor.transpose(bank[feat_bank[2 * c // NC]][0:EXP, at:at + CH], gate[:, c, :],
                                    ident[:, :]).then_inc(gt_mm, 1)
            pe.wait_ge(sel_ready, 1)

            def gate_rows(i):
                if i >= 2:
                    pe.wait_ge(wb_done, i - 1)
                ep, half = i % EP, i // EP
                pe.wait_ge(gate_split, half + 1)
                mm(bank[gate_bank[i % 2]][:, :], sel_r[:, 128 * ep:128 * ep + 128],
                   gate_hl[:, GT * half:GT * half + GT]).then_inc(wb_mm, 1)

            for i in range(EP):
                gate_rows(i)

            def layer2(m, bh, ep, free):
                pe.wait_ge(h1l_done, 4 * m + ep + 1)
                if free or ep >= 2:
                    pe.wait_ge(h2r_done, 4 * m + ep - 1)
                o = bank[z2_bank[ep % 2]][:, :]
                mm(o, w2_hi[:, ep, :], h1_hi[:, bh, ep, :], stop=False)
                mm(o, w2_lo[:, ep, :], h1_hi[:, bh, ep, :], start=False, stop=False)
                mm(o, w2_hi[:, ep, :], h1_lo[:, bh, ep, :], start=False).then_inc(z2_mm, 1)

            def layer3(m, bh, free):
                pe.wait_ge(h2w_done, 4 * m + 4)
                if free:
                    pe.wait_ge(yt_done, m)
                for ep in range(EP):
                    half = ep % 2
                    last = mm(bank[yt_bank][64 * half:64 * half + 64, :], wo_pair[:, ep, :], h2w[:, bh, ep, :],
                              start=(ep < 2), stop=(ep >= 2))
                last.then_inc(y_mm, 1)

            def fold_y(m, free):
                pe.wait_ge(yt_done, m + 1)
                if free:
                    pe.wait_ge(o_y, m)
                fold_rows(y_bank, lambda u: y_t[:, CH * u:CH * u + CH], yfold_mm)

            def expert_step(c, bh, kind):
                m = 2 * c + bh
                prev = not (kind == "first" and bh == 0)
                for ep in range(EP):
                    if not (kind == "last" and bh == 1):
                        layer1(m + 1, c + 1 if bh else c, 1 - bh, ep, True)
                    layer2(m, bh, ep, prev)
                    if not prev:
                        gate_rows(EP + ep)
                        if ep == EP - 1:
                            for n in range(NC):
                                mm(bank[y_bank][:, D * n:D * n + D], gate_t[:, CH * n:CH * n + CH],
                                   bo_sb[:, :]).then_inc(wbo_mm, 1)
                    if prev and ep == 1:
                        layer3(m - 1, 1 - bh, kind != "first")
                    if prev and ep == 3:
                        fold_y(m - 1, kind != "first")

            pe.wait_ge(xtl_done, NG + 1)
            pe.wait_ge(xth_done, NG)
            pe.wait_ge(w2_split, 2)
            pe.wait_ge(gt_done, 2)
            for bh in range(2):
                expert_step(0, bh, "first")
            with pe.Fori(1, NC - 1) as c:
                for bh in range(2):
                    expert_step(c, bh, "mid")
            for bh in range(2):
                expert_step(NC - 1, bh, "last")
            layer3(NG - 1, 1, True)
            fold_y(NG - 1, True)


_INS = ["x", "L0_tok_W", "L0_attn_Q", "L0_attn_E", "L0_ffn_Wr", "L0_ffn_br", "L0_ffn_W1", "L0_ffn_b1", "L0_ffn_g1",
        "L0_ffn_be1", "L0_ffn_m1", "L0_ffn_v1", "L0_ffn_W2", "L0_ffn_b2", "L0_ffn_g2", "L0_ffn_be2", "L0_ffn_m2",
        "L0_ffn_v2", "L0_ffn_Wo", "L0_ffn_bo"]


def _constants():
    import numpy as np
    t = np.array([[8 * q + 4 * half + s for q in range(2) for s in range(QS)] for half in range(2)])
    angle = 2 * np.pi * np.arange(FREQ)[:, None, None] * t[None] / PATCH
    dft = np.concatenate([np.cos(angle), -np.sin(angle)]) / np.sqrt(PATCH)
    ident = np.eye(128)
    mask = np.triu(np.ones((128, CH)))
    sel = np.zeros((GS, EXP * D))
    sel[:EXP] = sel[GS - EXP:] = np.repeat(np.eye(EXP), D, axis=1)
    fold = np.concatenate([np.eye(D), np.eye(D)])
    arrays = dict(dft=dft, ident=ident, mask=mask, sel=sel, fold=fold)
    return {n: a.astype(np.float32) for n, a in arrays.items()}


def kernel(**inputs):
    import numpy as np
    import concourse.bacc as bacc
    from concourse.bass_utils import run_bass_kernel_spmd

    nc = bacc.Bacc("TRN2", target_bir_lowering=False, num_devices=1)
    arrays, args = {}, []
    given = [(n, np.ascontiguousarray(inputs[n])) for n in _INS] + list(_constants().items())
    for name, a in given:
        arrays[f"in_{name}"] = a
        args.append(nc.dram_tensor(f"in_{name}", a.shape, mybir.dt.from_np(a.dtype), kind="ExternalInput").ap())
    result = nc.dram_tensor("result", (B, NTOK, D), mybir.dt.float32, kind="ExternalOutput").ap()
    build(nc, *args, result)
    r = run_bass_kernel_spmd(nc, [arrays], core_ids=[0])
    return r.results[0]["result"]
```
